# Optimizing a Trainium2 kernel written in Bass

```python
import numpy as np
import jax
import jax.numpy as jnp

def _softmax(x, axis=-1):
    return jax.nn.softmax(x, axis=axis)

def _gelu(x):
    return jax.nn.gelu(x, approximate=True)

def _silu(x):
    return jax.nn.silu(x)

def _sigmoid(x):
    return jax.nn.sigmoid(x)

def _layernorm(x, axis=-1, eps=1e-05):
    m = jnp.mean(x, axis=axis, keepdims=True)
    v = jnp.var(x, axis=axis, keepdims=True)
    return (x - m) / jnp.sqrt(v + eps)

def _scatter_add(tgt, idx, src, axis=0):
    return tgt.at[idx].add(src)

def _segment_sum(src, seg, n):
    return jax.ops.segment_sum(src, seg, n)
kernel_name = 'mk_adj_resnorm_d2_adj_r2_be95af'

def setup_inputs(seed: int=0):
    np.random.seed(seed)
    _w = jnp.asarray

    def _rec_inputs():
        import jax
        import jax.numpy as jnp
        _gk = jax.random.key(seed)
        x = -0.0004039 + 1 * jax.random.normal(jax.random.fold_in(_gk, 1), (64, 128, 384), jnp.float32)
        _a = jax.random.bernoulli(jax.random.fold_in(_gk, 2), 0.125, (64, 128, 128))
        _a = jnp.logical_or(_a, jnp.swapaxes(_a, -1, -2))
        _a = jnp.logical_or(_a, jnp.eye(128, dtype=bool))
        _af = _a.astype(jnp.float32)
        adj = _af
        return (x, adj)
    x, adj = _rec_inputs()

    def _L0_gnn_setup():
        import jax, jax.numpy as jnp
        import numpy as np
        B, S, H, L = (32, 256, 384, 2)

        def _layer_norm(z, a, b, eps=0.001):
            mu = jnp.mean(z, axis=-1, keepdims=True)
            sigma = jnp.std(z, axis=-1, keepdims=True, ddof=1)
            return (z - mu) / (sigma + eps) * a + b
        key = jax.random.key(seed)
        ks = jax.random.split(key, 6)
        hidden_state = jax.random.normal(ks[0], (B, S, H), dtype=jnp.float32)
        adjacency_matrix = (jax.random.uniform(ks[1], (B, S, S)) < 0.2).astype(jnp.float32)
        W_left = 0.05 * jax.random.normal(ks[2], (L, H, H), dtype=jnp.float32)
        W_right = 0.05 * jax.random.normal(ks[3], (L, H, H), dtype=jnp.float32)
        W_lin = 0.05 * jax.random.normal(ks[4], (L, H, H), dtype=jnp.float32)
        b_lin = jnp.zeros((L, H), dtype=jnp.float32)
        ln_a = jnp.ones((L, H), dtype=jnp.float32)
        ln_b = jnp.zeros((L, H), dtype=jnp.float32)
        return {'hidden_state': hidden_state, 'adjacency_matrix': adjacency_matrix, 'W_left': W_left, 'W_right': W_right, 'W_lin': W_lin, 'b_lin': b_lin, 'ln_a': ln_a, 'ln_b': ln_b}
    _L0_gnn_all = _L0_gnn_setup()
    _L0_gnn_in = {k: v for k, v in _L0_gnn_all.items() if k in ('W_left', 'W_right', 'W_lin', 'b_lin', 'ln_a', 'ln_b')}
    del _L0_gnn_all

    def _L1_gnn_setup():
        import jax, jax.numpy as jnp
        import numpy as np
        NUM_HEADS = 12
        HIDDEN = 384
        HEAD = HIDDEN // NUM_HEADS
        SCALE = HIDDEN ** (-0.5)
        key = jax.random.key(seed)
        ks = jax.random.split(key, 8)
        B, N = (16, 256)
        std = HIDDEN ** (-0.5)
        return {'x': jax.random.normal(ks[0], (B, N, HIDDEN), dtype=jnp.float32), 'encoding_bias': jax.random.normal(ks[1], (B, N, N), dtype=jnp.float32), 'Wq': jax.random.normal(ks[2], (HIDDEN, HIDDEN), dtype=jnp.float32) * std, 'Wk': jax.random.normal(ks[3], (HIDDEN, HIDDEN), dtype=jnp.float32) * std, 'Wv': jax.random.normal(ks[4], (HIDDEN, HIDDEN), dtype=jnp.float32) * std, 'bv': jax.random.normal(ks[5], (HIDDEN,), dtype=jnp.float32) * 0.01, 'Wo': jax.random.normal(ks[6], (HIDDEN, HIDDEN), dtype=jnp.float32) * std, 'bo': jax.random.normal(ks[7], (HIDDEN,), dtype=jnp.float32) * 0.01}
    _L1_gnn_all = _L1_gnn_setup()
    _L1_gnn_in = {k: v for k, v in _L1_gnn_all.items() if k in ('Wq', 'Wk', 'Wv', 'bv', 'Wo', 'bo')}
    del _L1_gnn_all
    return {'x': x, 'adj': adj, 'L0_gnn_W_left': _L0_gnn_in['W_left'], 'L0_gnn_W_right': _L0_gnn_in['W_right'], 'L0_gnn_W_lin': _L0_gnn_in['W_lin'], 'L0_gnn_b_lin': _L0_gnn_in['b_lin'], 'L0_gnn_ln_a': _L0_gnn_in['ln_a'], 'L0_gnn_ln_b': _L0_gnn_in['ln_b'], 'L1_gnn_Wq': _L1_gnn_in['Wq'], 'L1_gnn_Wk': _L1_gnn_in['Wk'], 'L1_gnn_Wv': _L1_gnn_in['Wv'], 'L1_gnn_bv': _L1_gnn_in['bv'], 'L1_gnn_Wo': _L1_gnn_in['Wo'], 'L1_gnn_bo': _L1_gnn_in['bo']}

def reference(x, adj, L0_gnn_W_left, L0_gnn_W_right, L0_gnn_W_lin, L0_gnn_b_lin, L0_gnn_ln_a, L0_gnn_ln_b, L1_gnn_Wq, L1_gnn_Wk, L1_gnn_Wv, L1_gnn_bv, L1_gnn_Wo, L1_gnn_bo):
    import jax
    import jax.numpy as jnp

    def _L0_gnn_ref(hidden_state, adjacency_matrix, W_left, W_right, W_lin, b_lin, ln_a, ln_b):
        import jax, jax.numpy as jnp
        import numpy as np
        B, S, H, L = (32, 256, 384, 2)

        def _layer_norm(z, a, b, eps=0.001):
            mu = jnp.mean(z, axis=-1, keepdims=True)
            sigma = jnp.std(z, axis=-1, keepdims=True, ddof=1)
            return (z - mu) / (sigma + eps) * a + b
        temper = float(np.sqrt(H))
        adj = adjacency_matrix
        adj_tri = jnp.triu(adj, k=1)
        diag_mask = jnp.triu(adj, k=0) - adj_tri
        h = hidden_state
        for l in range(L):
            m_left = jnp.einsum('bsh,oh->bso', h, W_left[l])
            m_right = jnp.einsum('bsh,oh->bso', h, W_right[l])
            u_left = jnp.einsum('bih,bjh->bij', h, m_left) / temper
            u_right = jnp.einsum('bih,bjh->bij', h, m_right) / temper
            u = u_left * adj_tri + u_left * diag_mask + u_right * jnp.swapaxes(adj_tri, 1, 2)
            delta_exp_u = jnp.exp(u) * adj
            attention = delta_exp_u / (jnp.sum(delta_exp_u, axis=2, keepdims=True) + 1e-10)
            h_lin = jnp.einsum('bsh,oh->bso', h, W_lin[l]) + b_lin[l]
            ctx = jnp.matmul(attention, h_lin)
            h = jax.nn.relu(_layer_norm(ctx, ln_a[l], ln_b[l]))
        return h

    def _L1_gnn_ref(x, encoding_bias, Wq, Wk, Wv, bv, Wo, bo):
        import jax, jax.numpy as jnp
        import numpy as np
        NUM_HEADS = 12
        HIDDEN = 384
        HEAD = HIDDEN // NUM_HEADS
        SCALE = HIDDEN ** (-0.5)
        B, N, _ = x.shape
        q = (x @ Wq.T).reshape(B, N, NUM_HEADS, HEAD)
        k = (x @ Wk.T).reshape(B, N, NUM_HEADS, HEAD)
        v = (x @ Wv.T + bv).reshape(B, N, NUM_HEADS, HEAD)
        a = jnp.einsum('bnhd,bmhd->bhnm', q, k) * SCALE + encoding_bias[:, None, :, :]
        pad_mask = jnp.all(a == 0, axis=-1)
        a = jnp.where(pad_mask[..., None], -jnp.inf, a)
        a = jax.nn.softmax(a, axis=-1)
        a = jnp.nan_to_num(a)
        o = jnp.einsum('bhnm,bmhd->bnhd', a, v).reshape(B, N, HIDDEN)
        return o @ Wo.T + bo
    x = _layernorm(x + _L0_gnn_ref(x, adj, L0_gnn_W_left, L0_gnn_W_right, L0_gnn_W_lin, L0_gnn_b_lin, L0_gnn_ln_a, L0_gnn_ln_b), axis=-1)
    x = _layernorm(x + _L1_gnn_ref(x, adj, L1_gnn_Wq, L1_gnn_Wk, L1_gnn_Wv, L1_gnn_bv, L1_gnn_Wo, L1_gnn_bo), axis=-1)
    return x

_drawn_inputs = setup_inputs


def setup_inputs(seed=0):
    import zlib

    import numpy as np

    out = dict(_drawn_inputs(seed))
    spreads = {'L0_gnn_b_lin': (0.0, 0.1), 'L0_gnn_ln_a': (1.0, 0.2), 'L0_gnn_ln_b': (0.0, 0.1)}
    factors = {'L1_gnn_Wq': 2.673, 'L1_gnn_Wk': 2.708, 'L1_gnn_bv': 5.753, 'L1_gnn_bo': 6.353}
    for name, (base, spread) in spreads.items():
        noise = np.random.default_rng([zlib.crc32(name.encode()), seed]).standard_normal(out[name].shape)
        drawn = base * np.exp(spread * noise) if base else spread * noise
        out[name] = jnp.asarray(drawn.astype(out[name].dtype))
    for name, factor in factors.items():
        out[name] = (out[name] * factor).astype(out[name].dtype)
    return out
```

```python
from contextlib import ExitStack

import concourse.bass as bass
from concourse import mybir
from concourse.alu_op_type import AluOpType as ALU

ACT = mybir.ActivationFunctionType
F32 = mybir.dt.float32
F16 = mybir.dt.float16
AX = mybir.AxisListType.X

P = 128
BU = 2
COLS = BU * P
HEADS = 12
GROUPS = 4
W_SCALE = 64.0

LEFT, RIGHT, LIN = (0, 3), (1, 4), (2, 5)
WQ, WK, WV, WO = 6, 7, 8, 9
MATS = 10
B_LIN, LN_A1, LN_B1, BV, BO = (0, 1), 2, 3, 4, 5
ROWS = 6


class Unit:

    def __init__(self, n, half, parity):
        self.n, self.half, self.parity = n, half, parity

    @property
    def first(self):
        return isinstance(self.n, int) and self.n == 0


def even(k):
    return Unit(2 * k, k, 0)


def odd(k):
    return Unit(2 * k + 1, k, 1)


class Steps:

    def __init__(self, sem, names):
        self.sem, self.names = sem, names

    def at(self, unit, name, back=0):
        return (unit.n - back) * len(self.names) + self.names.index(name) + 1


class Banks:

    def __init__(self, first, uses, by_act, by_dve, filled, act_took, dve_took):
        self.first, self.uses = first, uses
        self.filled = Steps(filled, uses)
        self.act_took = Steps(act_took, [u for u in uses if by_act(u)])
        self.dve_took = Steps(dve_took, [u for u in uses if by_dve(u)])

    def bank(self, use):
        return self.first + self.uses.index(use) % 4

    def before(self, use):
        k = self.uses.index(use)
        if k >= 4:
            return self.uses[k - 4], 0
        return [other for j, other in enumerate(self.uses) if j % 4 == k][-1], 1


def graph_net_kernel(nc, x, adj, weights, rows, cols, out):
    N, S, H = x.shape
    assert S == P and H % P == 0
    HC = H // P
    D = H // HEADS
    UNITS = N // BU
    LOOPS = (UNITS - 2) // 2
    assert UNITS == 2 * LOOPS + 2 and HC * GROUPS == HEADS and D * GROUPS == P
    TEMPER = float(H) ** 0.5
    SCALE = float(H) ** -0.5
    UNBIAS = (H / (H - 1.0)) ** 0.5

    x_u = x.rearrange("(u b) s h -> u s b h", b=BU)
    adj_u = adj.rearrange("(u b) s t -> u s b t", b=BU)
    out_u = out.rearrange("(u b) s h -> u s b h", b=BU)

    with ExitStack() as ctx:
        def sb(name, shape, dt=F32):
            return ctx.enter_context(nc.sbuf_tensor(name, shape, dt))

        def sem(name):
            return ctx.enter_context(nc.semaphore(name))

        psum = ctx.enter_context(nc.psum_tensor("psum", [P, 8, 512], F32))

        ident = sb("ident", [P, P])
        tri_left = sb("tri_left", [P, P])
        tri_right = sb("tri_right", [P, P])
        half_power = sb("half_power", [P, BU])
        minus_half_power = sb("minus_half_power", [P, BU])
        stage = sb("stage", [P, 3, HC * H])
        w_hi = sb("w_hi", [P, MATS, HC, H], F16)
        w_lo = sb("w_lo", [P, MATS, HC, H], F16)
        row = sb("row", [P, ROWS, H])
        ln_col = sb("ln_col", [P, 2, HC])

        x_nat = sb("x_nat", [P, 2, BU, H])
        adj_nat = sb("adj_nat", [P, 2, BU, P])
        hT_hi = sb("hT_hi", [P, HC, COLS], F16)
        hT_lo = sb("hT_lo", [P, HC, COLS], F16)
        adjT = sb("adjT", [P, BU, P])
        side_mask = sb("side_mask", [P, BU, 2, P])
        m_hi = sb("m_hi", [P, HC, 2, COLS], F16)
        m_lo = sb("m_lo", [P, HC, 2, COLS], F16)
        lin = sb("lin", [P, BU, H + 1])
        masked = sb("masked", [P, BU, 2, P])
        scoreT = sb("scoreT", [P, BU, P])
        expT = sb("expT", [P, BU, P])
        attT = sb("attT", [P, BU, P])
        z = sb("z", [P, BU, H])
        h_T = sb("h_T", [P, HC, COLS])
        scaled = sb("scaled", [P, BU, H])
        shifted = sb("shifted", [P, BU, H])
        y = sb("y", [P, BU, H])
        stats = sb("stats", [P, BU, 6])
        moments = sb("moments", [P, BU, 2])
        pause = sb("pause", [P, 1])
        eps_term = sb("eps_term", [P, BU])
        root = sb("root", [P, BU])
        spread = sb("spread", [P, BU])
        ln_scale = sb("ln_scale", [P, BU])
        ln_shift = sb("ln_shift", [P, BU])

        x1 = sb("x1", [P, BU, H])
        residual = sb("residual", [P, BU, H])
        xT_hi = sb("xT_hi", [P, HC, COLS], F16)
        xT_lo = sb("xT_lo", [P, HC, COLS], F16)
        qk_hi = sb("qk_hi", [P, HC, 2, COLS], F16)
        qk_lo = sb("qk_lo", [P, HC, 2, COLS], F16)
        v = sb("v", [P, BU, H])
        probs = sb("probs", [P, BU, HEADS, P])
        probsT = sb("probsT", [P, BU, HEADS, P])
        minus_max = sb("minus_max", [P, BU, HEADS])
        minimum = sb("minimum", [P, BU, HEADS])
        max_nonzero = sb("max_nonzero", [P, BU, HEADS])
        live = sb("live", [P, BU, HEADS])
        prob_sum = sb("prob_sum", [P, BU, HEADS])
        inverse_sum = sb("inverse_sum", [P, BU, HEADS])
        prob_scale = sb("prob_scale", [P, BU, HEADS])
        oT_hi = sb("oT_hi", [P, BU, HC, P], F16)
        oT_lo = sb("oT_lo", [P, BU, HC, P], F16)
        y2 = sb("y2", [P, BU, H])
        stats2 = sb("stats2", [P, BU, 6])
        moments2 = sb("moments2", [P, BU, 2])
        variance2 = sb("variance2", [P, BU])
        root2 = sb("root2", [P, BU])
        ln_shift2 = sb("ln_shift2", [P, BU])
        result = sb("result", [P, BU, H])

        x_loaded = [sem(f"x_loaded{p}") for p in range(2)]
        adj_loaded = [sem(f"adj_loaded{p}") for p in range(2)]
        weight_loaded = [sem(f"weight_loaded{k}") for k in range(3)]
        rows_loaded = sem("rows_loaded")
        weight_hi_ready = sem("weight_hi_ready")
        weight_ready = sem("weight_ready")
        const_set = sem("const_set")
        consts_ready = sem("consts_ready")
        rows_ready = sem("rows_ready")

        l0 = Banks(
            0,
            ["xT0", "xT1"]
            + [s for l in range(2) for s in (
                [f"m{l}_0", f"m{l}_1", f"m{l}_2", f"lin{l}_0", f"u{l}", f"lin{l}_1", f"ctx{l}_0", f"ctx{l}_1"]
                + (["hT0", "hT1"] if l == 0 else []))],
            lambda u: u[0] in "xmhc",
            lambda u: u[0] in "xmluc",
            sem("l0_filled"), sem("l0_act_took"), sem("l0_dve_took"))
        masks_ready = Steps(sem("masks_ready"), ["masks"])
        scores_ready = Steps(sem("scores_ready"), ["layer0", "layer1"])
        exp_ready = Steps(sem("exp_ready"), ["layer0", "layer1"])
        att_ready = Steps(sem("att_ready"), ["layer0", "layer1"])
        var_ready = Steps(sem("var_ready"), ["layer0", "layer1", "x1"])
        root_ready = Steps(sem("root_ready"), ["layer0", "layer1", "x1"])
        coef_ready = Steps(sem("coef_ready"), ["layer0", "layer1", "x1"])
        hT_ready = Steps(sem("hT_ready"), ["hi", "lo"])
        affine_step = Steps(sem("affine_step"), ["scaled", "shifted"])
        x1_ready = Steps(sem("x1_ready"), ["x1"])
        l0_own = Steps(sem("l0_own"), [f"{s}{l}" for l in range(2) for s in ("stats", "spread", "scale")]
                       + ["y", "ystats", "ymoments"])

        l1 = Banks(
            4,
            ["xT0", "xT1", "qk0", "qk1", "qk2"] + [f"s{b}_{g}" for b in range(BU) for g in range(GROUPS)]
            + ["v0", "v1"] + [f"pT{b}_{c}" for b in range(BU) for c in range(HC)] + ["oT0", "oT1", "y0", "y1"],
            lambda u: u[0] in "xqpo",
            lambda u: u[0] in "xqsvoy",
            sem("l1_filled"), sem("l1_act_took"), sem("l1_dve_took"))
        residual_ready = Steps(sem("residual_ready"), ["residual"])
        extrema_ready = Steps(sem("extrema_ready"), ["graph0", "graph1"])
        probs_ready = Steps(sem("probs_ready"), ["graph0", "graph1"])
        prob_scale_ready = Steps(sem("prob_scale_ready"), ["graph0", "graph1"])
        probs_scaled = Steps(sem("probs_scaled"), ["graph0", "graph1"])
        var2_ready = Steps(sem("var2_ready"), ["y2"])
        root2_ready = Steps(sem("root2_ready"), ["y2"])
        coef2_ready = Steps(sem("coef2_ready"), ["y2"])
        result_ready = Steps(sem("result_ready"), ["result"])
        result_stored = sem("result_stored")
        l1_own = Steps(sem("l1_own"), ["nonzero0", "live0", "nonzero1", "live1", "inverse0", "inverse1",
                                       "stats2", "moments2"])

        def loads(unit):
            return 16 * unit.half + 16

        def bank0(use, a=0, b=512):
            return psum[:, l0.bank(use), a:b]

        def bank1(use, a=0, b=512):
            return psum[:, l1.bank(use), a:b]

        block = ctx.enter_context(nc.Block())

        @block.sync
        def _(sp):
            def load_x(p, n):
                sp.dma_start(x_nat[:, p, :, :], x_u[n]).then_inc(x_loaded[p], 16)

            def load_adj(p, n):
                sp.dma_start(adj_nat[:, p, :, :], adj_u[n]).then_inc(adj_loaded[p], 16)

            def phase(a, b, load):
                if load:
                    sp.wait_ge(coef_ready.sem, coef_ready.at(b, "x1"))
                    load_x(1 - a.parity, a.n + 1)
                    sp.wait_ge(l1.dve_took.sem, l1.dve_took.at(b, "s1_3"))
                    load_adj(1 - a.parity, a.n + 1)
                sp.wait_ge(result_ready.sem, result_ready.at(b, "result"))
                sp.dma_start(out_u[b.n], result[:, :, :]).then_inc(result_stored, 16)

            load_x(0, 0)
            load_adj(0, 0)
            for w in range(MATS):
                if w >= 3:
                    sp.wait_ge(weight_ready, w - 2)
                sp.dma_start(stage[:, w % 3, :], weights[:, w]).then_inc(weight_loaded[w % 3], 16)
                if w == 1:
                    sp.dma_start(row[:, :, :], rows.partition_broadcast(P)).then_inc(rows_loaded, 16)
                    sp.dma_start(ln_col[:, :, :], cols).then_inc(rows_loaded, 16)
                if w == 2:
                    load_x(1, 1)
                    load_adj(1, 1)
            phase(odd(0), even(0), True)
            with sp.Fori(0, LOOPS - 1) as i:
                phase(even(i + 1), odd(i), True)
                phase(odd(i + 1), even(i + 1), True)
            phase(even(LOOPS), odd(LOOPS - 1), True)
            phase(odd(LOOPS), even(LOOPS), False)
            phase(None, odd(LOOPS), False)
            sp.wait_ge(result_stored, 16 * UNITS)

        @block.tensor
        def _(pe):
            def bank_free(banks, unit, use):
                old, back = banks.before(use)
                if back and unit.first:
                    return
                if old in banks.act_took.names:
                    pe.wait_ge(banks.act_took.sem, banks.act_took.at(unit, old, back))
                if old in banks.dve_took.names:
                    pe.wait_ge(banks.dve_took.sem, banks.dve_took.at(unit, old, back))

            def split_product(o, lhs, rhs, terms):
                last = None
                for t in range(terms):
                    for n, (lh, rh) in enumerate(((0, 0), (0, 1), (1, 0))):
                        last = pe.matmul(o, lhs(lh, t), rhs(rh, t), start=(t == 0 and n == 0),
                                         stop=(t == terms - 1 and n == 2))
                return last

            w_half, hT_half, m_half = (w_hi, w_lo), (hT_hi, hT_lo), (m_hi, m_lo)
            xT_half, qk_half, oT_half = (xT_hi, xT_lo), (qk_hi, qk_lo), (oT_hi, oT_lo)

            def transpose_rows(banks, unit, uses, source, extra=None):
                for k, use in enumerate(uses):
                    bank_free(banks, unit, use)
                    o = psum[:, banks.bank(use), :].rearrange("p (c b n) -> p c b n", c=2, b=BU)
                    for c in range(2 * k, min(2 * k + 2, HC)):
                        for b in range(BU):
                            last = pe.transpose(o[:, c % 2, b, :], source[:, b, c * P:(c + 1) * P], ident[:, :])
                    if k == 1 and extra is not None:
                        for b in range(BU):
                            last = pe.transpose(o[:, 1, b, :], extra[:, b, :], ident[:, :])
                    last.then_inc(banks.filled.sem, 1)

            def l0_xT(u):
                pe.wait_ge(x_loaded[u.parity], loads(u))
                pe.wait_ge(adj_loaded[u.parity], loads(u))
                transpose_rows(l0, u, ("xT0", "xT1"), x_nat[:, u.parity], adj_nat[:, u.parity])

            def l0_m(u, l, c):
                if c == 0 and l == 0:
                    pe.wait_ge(l0.act_took.sem, l0.act_took.at(u, "xT1"))
                    pe.wait_ge(l0.dve_took.sem, l0.dve_took.at(u, "xT1"))
                if c == 0 and l == 1:
                    pe.wait_ge(hT_ready.sem, hT_ready.at(u, "lo"))
                use = f"m{l}_{c}"
                bank_free(l0, u, use)
                for side, mat in enumerate((LEFT[l], RIGHT[l])):
                    last = split_product(bank0(use, side * COLS, (side + 1) * COLS),
                                         lambda h, t: w_half[h][:, mat, t, c * P:(c + 1) * P],
                                         lambda h, t: hT_half[h][:, t, :], HC)
                last.then_inc(l0.filled.sem, 1)

            def l0_lin(u, l, b):
                use = f"lin{l}_{b}"
                bank_free(l0, u, use)
                split_product(bank0(use, 0, H), lambda h, t: hT_half[h][:, t, b * P:(b + 1) * P],
                              lambda h, t: w_half[h][:, LIN[l], t, :], HC).then_inc(l0.filled.sem, 1)

            def l0_u(u, l):
                use = f"u{l}"
                pe.wait_ge(l0.act_took.sem, l0.act_took.at(u, f"m{l}_2"))
                pe.wait_ge(l0.dve_took.sem, l0.dve_took.at(u, f"m{l}_2"))
                bank_free(l0, u, use)
                for b in range(BU):
                    for side in range(2):
                        k = 2 * b + side
                        last = split_product(bank0(use, k * P, (k + 1) * P),
                                             lambda h, t: m_half[h][:, t, side, b * P:(b + 1) * P],
                                             lambda h, t: hT_half[h][:, t, b * P:(b + 1) * P], HC)
                last.then_inc(l0.filled.sem, 1)

            def l0_ctx(u, l):
                pe.wait_ge(att_ready.sem, att_ready.at(u, f"layer{l}"))
                pe.wait_ge(l0.dve_took.sem, l0.dve_took.at(u, f"lin{l}_1"))
                for b in range(BU):
                    use = f"ctx{l}_{b}"
                    bank_free(l0, u, use)
                    pe.matmul(bank0(use, 0, H + 1), attT[:, b, :], lin[:, b, :], start=True,
                              stop=True).then_inc(l0.filled.sem, 1)

            def l0_hT(u):
                pe.wait_ge(l0.act_took.sem, l0.act_took.at(u, "ctx0_1"))
                pe.wait_ge(l0.dve_took.sem, l0.dve_took.at(u, "ctx0_1"))
                transpose_rows(l0, u, ("hT0", "hT1"), z)

            def l1_xT(u):
                pe.wait_ge(x1_ready.sem, x1_ready.at(u, "x1"))
                transpose_rows(l1, u, ("xT0", "xT1"), x1)

            def l1_qk(u, c):
                if c == 0:
                    pe.wait_ge(l1.act_took.sem, l1.act_took.at(u, "xT1"))
                    pe.wait_ge(l1.dve_took.sem, l1.dve_took.at(u, "xT1"))
                use = f"qk{c}"
                bank_free(l1, u, use)
                for side, mat in enumerate((WQ, WK)):
                    last = split_product(bank1(use, side * COLS, (side + 1) * COLS),
                                         lambda h, t: w_half[h][:, mat, t, c * P:(c + 1) * P],
                                         lambda h, t: xT_half[h][:, t, :], HC)
                last.then_inc(l1.filled.sem, 1)

            def l1_s(u, b):
                if b == 0:
                    pe.wait_ge(l1.act_took.sem, l1.act_took.at(u, "qk2"))
                    pe.wait_ge(l1.dve_took.sem, l1.dve_took.at(u, "qk2"))
                for g0 in (0, 2):
                    for g in (g0, g0 + 1):
                        bank_free(l1, u, f"s{b}_{g}")
                    for c in range(HC):
                        for n, (lh, rh) in enumerate(((0, 0), (0, 1), (1, 0))):
                            for g in (g0, g0 + 1):
                                use = f"s{b}_{g}"
                                r = slice(g * D, (g + 1) * D)
                                mm = pe.matmul(bank1(use, c * P, (c + 1) * P),
                                               qk_half[lh][r, c, 0, b * P:(b + 1) * P],
                                               qk_half[rh][r, c, 1, b * P:(b + 1) * P],
                                               start=(n == 0), stop=(n == 2))
                                if c == HC - 1 and n == 2:
                                    mm.then_inc(l1.filled.sem, 1)

            def l1_v(u, b):
                use = f"v{b}"
                bank_free(l1, u, use)
                split_product(bank1(use, 0, H), lambda h, t: xT_half[h][:, t, b * P:(b + 1) * P],
                              lambda h, t: w_half[h][:, WV, t, :], HC).then_inc(l1.filled.sem, 1)

            def l1_pT(u, b):
                pe.wait_ge(probs_scaled.sem, probs_scaled.at(u, f"graph{b}"))
                for c in range(HC):
                    use = f"pT{b}_{c}"
                    bank_free(l1, u, use)
                    for k in range(4):
                        last = pe.transpose(bank1(use, k * P, (k + 1) * P), probs[:, b, 4 * c + k, :], ident[:, :])
                    last.then_inc(l1.filled.sem, 1)

            def l1_oT(u, b):
                use = f"oT{b}"
                pe.wait_ge(l1.act_took.sem, l1.act_took.at(u, f"pT{b}_{HC - 1}"))
                if b == 0:
                    pe.wait_ge(l1.dve_took.sem, l1.dve_took.at(u, "v1"))
                bank_free(l1, u, use)
                for c in range(HC):
                    for g in range(GROUPS):
                        head = c * GROUPS + g
                        last = pe.matmul(psum[g * D:(g + 1) * D, l1.bank(use), c * P:(c + 1) * P],
                                         v[:, b, head * D:(head + 1) * D], probsT[:, b, g * HC + c, :],
                                         start=True, stop=True)
                last.then_inc(l1.filled.sem, 1)

            def l1_y(u, b):
                use = f"y{b}"
                pe.wait_ge(l1.act_took.sem, l1.act_took.at(u, f"oT{b}"))
                pe.wait_ge(l1.dve_took.sem, l1.dve_took.at(u, f"oT{b}"))
                bank_free(l1, u, use)
                split_product(bank1(use, 0, H), lambda h, t: oT_half[h][:, b, t, :],
                              lambda h, t: w_half[h][:, WO, t, :], HC).then_inc(l1.filled.sem, 1)

            def phase(a, b):
                l0_xT(a)
                l0_m(a, 0, 0)
                l0_m(a, 0, 1)
                l1_xT(b)
                l0_m(a, 0, 2)
                l1_qk(b, 0)
                l0_lin(a, 0, 0)
                l1_qk(b, 1)
                l0_u(a, 0)
                l1_qk(b, 2)
                l0_lin(a, 0, 1)
                l0_ctx(a, 0)
                l1_s(b, 0)
                l1_s(b, 1)
                l0_hT(a)
                l1_v(b, 0)
                l1_v(b, 1)
                for c in range(HC):
                    l0_m(a, 1, c)
                l0_lin(a, 1, 0)
                l0_u(a, 1)
                l0_lin(a, 1, 1)
                l1_pT(b, 0)
                l0_ctx(a, 1)
                l1_pT(b, 1)
                l1_oT(b, 0)
                l1_oT(b, 1)
                l1_y(b, 0)
                l1_y(b, 1)

            pe.wait_ge(consts_ready, 1)
            a = even(0)
            l0_xT(a)
            for l in range(2):
                pe.wait_ge(weight_ready, LIN[l])
                for c in range(HC):
                    l0_m(a, l, c)
                pe.wait_ge(weight_ready, LIN[l] + 1)
                l0_lin(a, l, 0)
                l0_u(a, l)
                l0_lin(a, l, 1)
                l0_ctx(a, l)
                if l == 0:
                    l0_hT(a)
            pe.wait_ge(weight_ready, MATS)
            phase(odd(0), even(0))
            with pe.Fori(0, LOOPS) as i:
                phase(even(i + 1), odd(i))
                phase(odd(i + 1), even(i + 1))
            b = odd(LOOPS)
            l1_xT(b)
            for c in range(HC):
                l1_qk(b, c)
            l1_s(b, 0)
            l1_s(b, 1)
            l1_v(b, 0)
            l1_v(b, 1)
            l1_pT(b, 0)
            l1_pT(b, 1)
            l1_oT(b, 0)
            l1_oT(b, 1)
            l1_y(b, 0)
            l1_y(b, 1)

        @block.scalar
        def _(act):
            def flat(t, k, n):
                return t[:, 2 * k:2 * k + n, :].rearrange("p c n -> p (c n)")

            def weight_high(w):
                act.wait_ge(weight_loaded[w % 3], 16 * (w // 3) + 16)
                act.activation(w_hi[:, w].rearrange("p c n -> p (c n)"), stage[:, w % 3, :], ACT.Copy,
                               scale=W_SCALE).then_inc(weight_hi_ready, 1)

            def l0_xT(u):
                act.wait_ge(l0.filled.sem, l0.filled.at(u, "xT0"))
                act.activation(flat(hT_hi, 0, 2), bank0("xT0"), ACT.Copy).then_inc(l0.act_took.sem, 1)
                act.wait_ge(l0.filled.sem, l0.filled.at(u, "xT1"))
                act.activation(flat(hT_hi, 1, 1), bank0("xT1", 0, COLS), ACT.Copy)
                act.activation(adjT[:, :, :].rearrange("p b n -> p (b n)"), bank0("xT1", COLS), ACT.Copy)\
                   .then_inc(l0.act_took.sem, 1)

            def l0_m(u, l, c):
                act.wait_ge(l0.filled.sem, l0.filled.at(u, f"m{l}_{c}"))
                act.activation(m_hi[:, c].rearrange("p s n -> p (s n)"), bank0(f"m{l}_{c}"), ACT.Copy)\
                   .then_inc(l0.act_took.sem, 1)

            def l0_exp(u, l):
                act.wait_ge(scores_ready.sem, scores_ready.at(u, f"layer{l}"))
                act.activation(expT[:, :, :], scoreT[:, :, :], ACT.Exp, scale=1.0 / (W_SCALE * TEMPER))\
                   .then_inc(exp_ready.sem, 1)

            def l0_norm(u, l):
                act.wait_ge(coef_ready.sem, coef_ready.at(u, f"layer{l}"))
                for b in range(BU):
                    act.activation(z[:, b, :], bank0(f"ctx{l}_{b}", 0, H), ACT.Identity,
                                   bias=ln_shift[:, b:b + 1], scale=ln_scale[:, b:b + 1])\
                       .then_inc(l0.act_took.sem, 1)

            def l0_hT(u):
                for k, use in enumerate(("hT0", "hT1")):
                    act.wait_ge(l0.filled.sem, l0.filled.at(u, use))
                    for c in range(2 * k, min(2 * k + 2, HC)):
                        last = act.activation(h_T[:, c, :], bank0(use, c % 2 * COLS, (c % 2 + 1) * COLS), ACT.Relu,
                                              bias=ln_col[:, 1, c:c + 1], scale=ln_col[:, 0, c:c + 1])
                    last.then_inc(l0.act_took.sem, 1)

            def l0_x1(u):
                act.wait_ge(coef_ready.sem, coef_ready.at(u, "x1"))
                for b in range(BU):
                    last = act.activation(x1[:, b, :], y[:, b, :], ACT.Identity,
                                          bias=ln_shift[:, b:b + 1], scale=ln_scale[:, b:b + 1])
                last.then_inc(x1_ready.sem, 1)

            def l1_xT(u):
                for k, use in enumerate(("xT0", "xT1")):
                    n = 2 - k
                    act.wait_ge(l1.filled.sem, l1.filled.at(u, use))
                    act.activation(flat(xT_hi, k, n), bank1(use, 0, n * COLS), ACT.Copy).then_inc(l1.act_took.sem, 1)

            def l1_qk(u, c):
                act.wait_ge(l1.filled.sem, l1.filled.at(u, f"qk{c}"))
                act.activation(qk_hi[:, c].rearrange("p s n -> p (s n)"), bank1(f"qk{c}"), ACT.Copy)\
                   .then_inc(l1.act_took.sem, 1)

            def l1_exp(u, b, part):
                if part == 0:
                    act.wait_ge(extrema_ready.sem, extrema_ready.at(u, f"graph{b}"))
                for k in range(6 * part, 6 * part + 6):
                    last = act.activation(probs[:, b, k, :], probs[:, b, k, :], ACT.Exp,
                                          bias=minus_max[:, b, k:k + 1], accum_out=prob_sum[:, b, k:k + 1])
                if part == 1:
                    last.then_inc(probs_ready.sem, 1)

            def l1_pT(u, b):
                for c in range(HC):
                    act.wait_ge(l1.filled.sem, l1.filled.at(u, f"pT{b}_{c}"))
                    act.activation(probsT[:, b, 4 * c:4 * c + 4, :].rearrange("p k n -> p (k n)"),
                                   bank1(f"pT{b}_{c}"), ACT.Copy).then_inc(l1.act_took.sem, 1)

            def l1_oT(u, b):
                act.wait_ge(l1.filled.sem, l1.filled.at(u, f"oT{b}"))
                act.activation(oT_hi[:, b].rearrange("p c n -> p (c n)"), bank1(f"oT{b}", 0, H), ACT.Copy)\
                   .then_inc(l1.act_took.sem, 1)

            def l1_result(u):
                act.wait_ge(coef2_ready.sem, coef2_ready.at(u, "y2"))
                if not u.first:
                    act.wait_ge(result_stored, 16 * u.n)
                for b in range(BU):
                    last = act.activation(result[:, b, :], y2[:, b, :], ACT.Identity,
                                          bias=ln_shift2[:, b:b + 1], scale=root2[:, b:b + 1])
                last.then_inc(result_ready.sem, 1)

            def phase(a, b):
                l0_xT(a)
                l0_m(a, 0, 0)
                l0_m(a, 0, 1)
                l1_xT(b)
                l0_m(a, 0, 2)
                l1_qk(b, 0)
                l1_qk(b, 1)
                l0_exp(a, 0)
                l1_qk(b, 2)
                l0_norm(a, 0)
                l0_hT(a)
                l1_exp(b, 0, 0)
                l0_m(a, 1, 0)
                l1_exp(b, 0, 1)
                l0_m(a, 1, 1)
                l1_exp(b, 1, 0)
                l0_m(a, 1, 2)
                l1_exp(b, 1, 1)
                l0_exp(a, 1)
                l1_pT(b, 0)
                l0_norm(a, 1)
                l1_pT(b, 1)
                l1_oT(b, 0)
                l1_oT(b, 1)
                l0_x1(a)
                l1_result(b)

            for w in range(3):
                weight_high(w)
            act.wait_ge(rows_loaded, 32)
            a = even(0)
            l0_xT(a)
            for c in range(HC):
                l0_m(a, 0, c)
            for w in range(3, 6):
                weight_high(w)
            l0_exp(a, 0)
            l0_norm(a, 0)
            l0_hT(a)
            for c in range(HC):
                l0_m(a, 1, c)
            for w in range(6, MATS):
                weight_high(w)
            l0_exp(a, 1)
            l0_norm(a, 1)
            l0_x1(a)
            phase(odd(0), even(0))
            with act.Fori(0, LOOPS) as i:
                phase(even(i + 1), odd(i))
                phase(odd(i + 1), even(i + 1))
            b = odd(LOOPS)
            l1_xT(b)
            for c in range(HC):
                l1_qk(b, c)
            for g in range(BU):
                l1_exp(b, g, 0)
                l1_exp(b, g, 1)
            l1_pT(b, 0)
            l1_pT(b, 1)
            l1_oT(b, 0)
            l1_oT(b, 1)
            l1_result(b)

        @block.vector
        def _(dve):
            def flat(t, k, n):
                return t[:, 2 * k:2 * k + n, :].rearrange("p c n -> p (c n)")

            def weight_low(w):
                dve.wait_ge(weight_hi_ready, w + 1)
                dve.scalar_tensor_tensor(out=w_lo[:, w].rearrange("p c n -> p (c n)"), in0=stage[:, w % 3, :],
                                         scalar=W_SCALE, in1=w_hi[:, w].rearrange("p c n -> p (c n)"),
                                         op0=ALU.mult, op1=ALU.subtract).then_inc(weight_ready, 1)

            def low_half(banks, unit, use, lo, hi, n):
                dve.wait_ge(banks.act_took.sem, banks.act_took.at(unit, use))
                dve.tensor_tensor(lo, psum[:, banks.bank(use), 0:n], hi, ALU.subtract)\
                   .then_inc(banks.dve_took.sem, 1)

            def l0_xT(u):
                for k, use in enumerate(("xT0", "xT1")):
                    low_half(l0, u, use, flat(hT_lo, k, 2 - k), flat(hT_hi, k, 2 - k), (2 - k) * COLS)

            def l0_m(u, l, c):
                low_half(l0, u, f"m{l}_{c}", m_lo[:, c].rearrange("p s n -> p (s n)"),
                         m_hi[:, c].rearrange("p s n -> p (s n)"), 2 * COLS)

            def l0_lin(u, l, b):
                dve.wait_ge(l0.filled.sem, l0.filled.at(u, f"lin{l}_{b}"))
                dve.tensor_tensor(lin[:, b, 0:H], bank0(f"lin{l}_{b}", 0, H), row[:, B_LIN[l], :], ALU.add)\
                   .then_inc(l0.dve_took.sem, 1)

            def l0_scores(u, l):
                if l == 0:
                    dve.wait_ge(masks_ready.sem, masks_ready.at(u, "masks"))
                dve.wait_ge(l0.filled.sem, l0.filled.at(u, f"u{l}"))
                dve.tensor_tensor(masked[:, :, :, :].rearrange("p b s n -> p (b s n)"), bank0(f"u{l}"),
                                  side_mask[:, :, :, :].rearrange("p b s n -> p (b s n)"), ALU.mult)\
                   .then_inc(l0.dve_took.sem, 1)
                dve.wait_ge(l0.dve_took.sem, l0.dve_took.at(u, f"u{l}"))
                dve.tensor_tensor(scoreT[:, :, :], masked[:, :, 0, :], masked[:, :, 1, :], ALU.add)\
                   .then_inc(scores_ready.sem, 1)

            def l0_att(u, l):
                dve.wait_ge(exp_ready.sem, exp_ready.at(u, f"layer{l}"))
                dve.tensor_tensor(attT[:, :, :], expT[:, :, :], adjT[:, :, :], ALU.mult).then_inc(att_ready.sem, 1)

            def l0_stats(u, l):
                for b in range(BU):
                    dve.wait_ge(l0.filled.sem, l0.filled.at(u, f"ctx{l}_{b}"))
                    last = dve.bn_stats(stats[:, b, :], bank0(f"ctx{l}_{b}", 0, H))
                    if b == BU - 1:
                        last.then_inc(l0_own.sem, 1)
                    dve.tensor_scalar(eps_term[:, b:b + 1], bank0(f"ctx{l}_{b}", H, H + 1), 1e-3,
                                      W_SCALE * 1e-3 * 1e-10, ALU.mult, ALU.add).then_inc(l0.dve_took.sem, 1)
                moments_of(l0_own, u, f"stats{l}", stats, moments, var_ready.sem)

            def moments_of(own, u, step, source, target, done):
                dve.wait_ge(own.sem, own.at(u, step))
                dve.memset(pause[:, :], 0.0)
                for b in range(BU):
                    last = dve.bn_aggr(target[:, b, :], source[:, b, :])
                last.then_inc(done, 1)

            def l0_coef(u, l):
                dve.wait_ge(root_ready.sem, root_ready.at(u, f"layer{l}"))
                dve.wait_ge(l0.dve_took.sem, l0.dve_took.at(u, f"ctx{l}_1"))
                dve.scalar_tensor_tensor(out=spread[:, :], in0=root[:, :], scalar=UNBIAS, in1=eps_term[:, :],
                                         op0=ALU.mult, op1=ALU.add).then_inc(l0_own.sem, 1)
                dve.wait_ge(l0_own.sem, l0_own.at(u, f"spread{l}"))
                dve.reciprocal(ln_scale[:, :], spread[:, :]).then_inc(l0_own.sem, 1)
                dve.wait_ge(l0_own.sem, l0_own.at(u, f"scale{l}"))
                dve.scalar_tensor_tensor(out=ln_shift[:, :], in0=moments[:, :, 0], scalar=-1.0, in1=ln_scale[:, :],
                                         op0=ALU.mult, op1=ALU.mult).then_inc(coef_ready.sem, 1)

            def l0_hT(u):
                dve.wait_ge(l0.act_took.sem, l0.act_took.at(u, "hT1"))
                dve.tensor_copy(hT_hi[:, :, :], h_T[:, :, :]).then_inc(hT_ready.sem, 1)
                dve.wait_ge(hT_ready.sem, hT_ready.at(u, "hi"))
                dve.tensor_tensor(hT_lo[:, :, :], h_T[:, :, :], hT_hi[:, :, :], ALU.subtract)\
                   .then_inc(hT_ready.sem, 1)

            def l0_y(u):
                dve.wait_ge(affine_step.sem, affine_step.at(u, "shifted"))
                dve.scalar_tensor_tensor(out=y[:, :, :], in0=shifted[:, :, :], scalar=0.0,
                                         in1=x_nat[:, u.parity, :, :], op0=ALU.max, op1=ALU.add)\
                   .then_inc(l0_own.sem, 1)
                dve.wait_ge(l0_own.sem, l0_own.at(u, "y"))
                for b in range(BU):
                    last = dve.bn_stats(stats[:, b, :], y[:, b, :])
                last.then_inc(l0_own.sem, 1)
                moments_of(l0_own, u, "ystats", stats, moments, l0_own.sem)
                dve.wait_ge(l0_own.sem, l0_own.at(u, "ymoments"))
                dve.tensor_scalar(spread[:, :], moments[:, :, 1], 1e-5, None, ALU.add).then_inc(var_ready.sem, 1)

            def l0_y_coef(u):
                dve.wait_ge(root_ready.sem, root_ready.at(u, "x1"))
                dve.tensor_copy(ln_scale[:, :], root[:, :])
                dve.scalar_tensor_tensor(out=ln_shift[:, :], in0=moments[:, :, 0], scalar=-1.0, in1=root[:, :],
                                         op0=ALU.mult, op1=ALU.mult).then_inc(coef_ready.sem, 1)

            def l1_xT(u):
                for k, use in enumerate(("xT0", "xT1")):
                    low_half(l1, u, use, flat(xT_lo, k, 2 - k), flat(xT_hi, k, 2 - k), (2 - k) * COLS)

            def l1_qk(u, c):
                low_half(l1, u, f"qk{c}", qk_lo[:, c].rearrange("p s n -> p (s n)"),
                         qk_hi[:, c].rearrange("p s n -> p (s n)"), 2 * COLS)

            def l1_scores(u, b):
                if b == 0:
                    dve.wait_ge(adj_loaded[u.parity], loads(u))
                bias = adj_nat[:, u.parity, b, :].unsqueeze(1).to_broadcast([P, HC, P])
                for g in range(GROUPS):
                    use = f"s{b}_{g}"
                    dve.wait_ge(l1.filled.sem, l1.filled.at(u, use))
                    dve.scalar_tensor_tensor(out=probs[:, b, g * HC:(g + 1) * HC, :],
                                             in0=bank1(use, 0, H).rearrange("p (c n) -> p c n", c=HC),
                                             scalar=SCALE / (W_SCALE * W_SCALE), in1=bias,
                                             op0=ALU.mult, op1=ALU.add).then_inc(l1.dve_took.sem, 1)

            def l1_extrema(u, b):
                dve.wait_ge(l1.dve_took.sem, l1.dve_took.at(u, f"s{b}_3"))
                dve.tensor_reduce(minus_max[:, b, :], probs[:, b, :, :], AX, ALU.max, negate=True)
                dve.tensor_reduce(minimum[:, b, :], probs[:, b, :, :], AX, ALU.min)\
                   .then_inc(extrema_ready.sem, 1)
                dve.wait_ge(extrema_ready.sem, extrema_ready.at(u, f"graph{b}"))
                dve.tensor_scalar(max_nonzero[:, b, :], minus_max[:, b, :], 0.0, None, ALU.not_equal)\
                   .then_inc(l1_own.sem, 1)
                dve.wait_ge(l1_own.sem, l1_own.at(u, f"nonzero{b}"))
                dve.scalar_tensor_tensor(out=live[:, b, :], in0=minimum[:, b, :], scalar=0.0,
                                         in1=max_nonzero[:, b, :], op0=ALU.not_equal, op1=ALU.max)\
                   .then_inc(l1_own.sem, 1)

            def l1_prob_scale(u, b):
                dve.wait_ge(probs_ready.sem, probs_ready.at(u, f"graph{b}"))
                dve.reciprocal(inverse_sum[:, b, :], prob_sum[:, b, :]).then_inc(l1_own.sem, 1)
                dve.wait_ge(l1_own.sem, l1_own.at(u, f"inverse{b}"))
                dve.scalar_tensor_tensor(out=prob_scale[:, b, :], in0=live[:, b, :], scalar=1.0 / W_SCALE,
                                         in1=inverse_sum[:, b, :], op0=ALU.mult, op1=ALU.mult)\
                   .then_inc(prob_scale_ready.sem, 1)

            def l1_v(u, b):
                dve.wait_ge(l1.filled.sem, l1.filled.at(u, f"v{b}"))
                dve.tensor_tensor(v[:, b, :], bank1(f"v{b}", 0, H), row[:, BV, :], ALU.add)\
                   .then_inc(l1.dve_took.sem, 1)

            def l1_oT(u, b):
                low_half(l1, u, f"oT{b}", oT_lo[:, b].rearrange("p c n -> p (c n)"),
                         oT_hi[:, b].rearrange("p c n -> p (c n)"), H)

            def l1_y(u, b):
                if b == 0:
                    dve.wait_ge(residual_ready.sem, residual_ready.at(u, "residual"))
                dve.wait_ge(l1.filled.sem, l1.filled.at(u, f"y{b}"))
                dve.scalar_tensor_tensor(out=y2[:, b, :], in0=bank1(f"y{b}", 0, H), scalar=1.0 / W_SCALE,
                                         in1=residual[:, b, :], op0=ALU.mult, op1=ALU.add)\
                   .then_inc(l1.dve_took.sem, 1)

            def l1_stats(u):
                dve.wait_ge(l1.dve_took.sem, l1.dve_took.at(u, "y1"))
                for b in range(BU):
                    last = dve.bn_stats(stats2[:, b, :], y2[:, b, :])
                last.then_inc(l1_own.sem, 1)
                moments_of(l1_own, u, "stats2", stats2, moments2, l1_own.sem)
                dve.wait_ge(l1_own.sem, l1_own.at(u, "moments2"))
                dve.tensor_scalar(variance2[:, :], moments2[:, :, 1], 1e-5, None, ALU.add)\
                   .then_inc(var2_ready.sem, 1)

            def l1_coef(u):
                dve.wait_ge(root2_ready.sem, root2_ready.at(u, "y2"))
                dve.scalar_tensor_tensor(out=ln_shift2[:, :], in0=moments2[:, :, 0], scalar=-1.0, in1=root2[:, :],
                                         op0=ALU.mult, op1=ALU.mult).then_inc(coef2_ready.sem, 1)

            def phase(a, b):
                l0_xT(a)
                l0_m(a, 0, 0)
                l0_m(a, 0, 1)
                l1_xT(b)
                l0_m(a, 0, 2)
                l1_qk(b, 0)
                l0_lin(a, 0, 0)
                l1_qk(b, 1)
                l0_scores(a, 0)
                l1_qk(b, 2)
                l0_att(a, 0)
                l0_lin(a, 0, 1)
                l0_stats(a, 0)
                l1_scores(b, 0)
                l0_coef(a, 0)
                l1_extrema(b, 0)
                l1_scores(b, 1)
                l0_hT(a)
                l1_v(b, 0)
                l1_v(b, 1)
                l0_m(a, 1, 0)
                l1_extrema(b, 1)
                l0_m(a, 1, 1)
                l0_m(a, 1, 2)
                l1_prob_scale(b, 0)
                l0_lin(a, 1, 0)
                l0_scores(a, 1)
                l0_lin(a, 1, 1)
                l1_prob_scale(b, 1)
                l0_att(a, 1)
                l0_stats(a, 1)
                l0_coef(a, 1)
                l1_oT(b, 0)
                l1_oT(b, 1)
                l1_y(b, 0)
                l0_y(a)
                l1_y(b, 1)
                l0_y_coef(a)
                l1_stats(b)
                l1_coef(b)

            dve.memset(lin[:, :, H:H + 1], W_SCALE)
            for w in range(3):
                weight_low(w)
            dve.wait_ge(rows_loaded, 32)
            for r in (*B_LIN, BV):
                last = dve.tensor_scalar(row[:, r, :], row[:, r, :], W_SCALE, None, ALU.mult)
            last.then_inc(rows_ready, 1)
            dve.wait_ge(rows_ready, 1)
            a = even(0)
            l0_xT(a)
            for c in range(HC):
                l0_m(a, 0, c)
            for w in range(3, 6):
                weight_low(w)
            for l in range(2):
                if l == 1:
                    for c in range(HC):
                        l0_m(a, 1, c)
                    for w in range(6, MATS):
                        weight_low(w)
                l0_lin(a, l, 0)
                l0_scores(a, l)
                l0_lin(a, l, 1)
                l0_att(a, l)
                l0_stats(a, l)
                l0_coef(a, l)
                if l == 0:
                    l0_hT(a)
            l0_y(a)
            l0_y_coef(a)
            phase(odd(0), even(0))
            with dve.Fori(0, LOOPS) as i:
                phase(even(i + 1), odd(i))
                phase(odd(i + 1), even(i + 1))
            b = odd(LOOPS)
            l1_xT(b)
            for c in range(HC):
                l1_qk(b, c)
            for g in range(BU):
                l1_scores(b, g)
                l1_extrema(b, g)
            l1_v(b, 0)
            l1_v(b, 1)
            l1_prob_scale(b, 0)
            l1_prob_scale(b, 1)
            l1_oT(b, 0)
            l1_oT(b, 1)
            l1_y(b, 0)
            l1_y(b, 1)
            l1_stats(b)
            l1_coef(b)

        @block.gpsimd
        def _(pool):
            def l0_masks(u):
                pool.wait_ge(l0.act_took.sem, l0.act_took.at(u, "xT1"))
                pool.tensor_tensor(side_mask[:, :, 0, :], adjT[:, :, :],
                                   tri_left[:, :].unsqueeze(1).to_broadcast([P, BU, P]), ALU.mult)
                pool.tensor_tensor(side_mask[:, :, 1, :], adj_nat[:, u.parity, :, :],
                                   tri_right[:, :].unsqueeze(1).to_broadcast([P, BU, P]), ALU.mult)\
                    .then_inc(masks_ready.sem, 1)

            def l0_root(u, l):
                pool.wait_ge(var_ready.sem, var_ready.at(u, f"layer{l}"))
                pool.tensor_tensor(root[:, :], moments[:, :, 1], half_power[:, :], ALU.pow)\
                    .then_inc(root_ready.sem, 1)

            def l0_affine(u):
                pool.wait_ge(l0.act_took.sem, l0.act_took.at(u, "ctx1_1"))
                pool.tensor_tensor(scaled[:, :, :], z[:, :, :],
                                   row[:, LN_A1:LN_A1 + 1, :].to_broadcast([P, BU, H]), ALU.mult)\
                    .then_inc(affine_step.sem, 1)
                pool.wait_ge(affine_step.sem, affine_step.at(u, "scaled"))
                pool.tensor_tensor(shifted[:, :, :], scaled[:, :, :],
                                   row[:, LN_B1:LN_B1 + 1, :].to_broadcast([P, BU, H]), ALU.add)\
                    .then_inc(affine_step.sem, 1)

            def l0_y_root(u):
                pool.wait_ge(var_ready.sem, var_ready.at(u, "x1"))
                pool.tensor_tensor(root[:, :], spread[:, :], minus_half_power[:, :], ALU.pow)\
                    .then_inc(root_ready.sem, 1)

            def l1_residual(u):
                pool.wait_ge(x1_ready.sem, x1_ready.at(u, "x1"))
                if not u.first:
                    pool.wait_ge(l1.dve_took.sem, l1.dve_took.at(u, "y1", back=1))
                pool.tensor_tensor(residual[:, :, :], x1[:, :, :],
                                   row[:, BO:BO + 1, :].to_broadcast([P, BU, H]), ALU.add)\
                    .then_inc(residual_ready.sem, 1)

            def l1_scale_probs(u, b):
                pool.wait_ge(prob_scale_ready.sem, prob_scale_ready.at(u, f"graph{b}"))
                pool.tensor_tensor(probs[:, b, :, :], probs[:, b, :, :],
                                   prob_scale[:, b, :].unsqueeze(2).to_broadcast([P, HEADS, P]), ALU.mult)\
                    .then_inc(probs_scaled.sem, 1)

            def l1_root(u):
                pool.wait_ge(var2_ready.sem, var2_ready.at(u, "y2"))
                pool.tensor_tensor(root2[:, :], variance2[:, :], minus_half_power[:, :], ALU.pow)\
                    .then_inc(root2_ready.sem, 1)

            def phase(a, b):
                l0_masks(a)
                l1_residual(b)
                l0_root(a, 0)
                l1_scale_probs(b, 0)
                l1_scale_probs(b, 1)
                l0_root(a, 1)
                l0_affine(a)
                l0_y_root(a)
                l1_root(b)

            pool.memset(ident[:, :], 0.0)
            pool.memset(tri_left[:, :], 1.0)
            pool.memset(tri_right[:, :], 1.0)
            pool.memset(half_power[:, :], 0.5)
            pool.memset(minus_half_power[:, :], -0.5).then_inc(const_set, 1)
            pool.wait_ge(const_set, 1)
            pool.affine_select(out=tri_left[:, :], in_=tri_left[:, :], compare_op=ALU.is_ge, fill=0.0, base=0,
                               pattern=[[-1, P]], channel_multiplier=1)
            pool.affine_select(out=tri_right[:, :], in_=tri_right[:, :], compare_op=ALU.is_gt, fill=0.0, base=0,
                               pattern=[[1, P]], channel_multiplier=-1)
            pool.affine_select(out=ident[:, :], in_=ident[:, :], compare_op=ALU.not_equal, fill=1.0, base=0,
                               pattern=[[-1, P]], channel_multiplier=1).then_inc(consts_ready, 1)
            pool.wait_ge(consts_ready, 1)
            a = even(0)
            pool.wait_ge(rows_ready, 1)
            pool.wait_ge(adj_loaded[a.parity], loads(a))
            l0_masks(a)
            l0_root(a, 0)
            l0_root(a, 1)
            l0_affine(a)
            l0_y_root(a)
            phase(odd(0), even(0))
            with pool.Fori(0, LOOPS) as i:
                phase(even(i + 1), odd(i))
                phase(odd(i + 1), even(i + 1))
            b = odd(LOOPS)
            l1_residual(b)
            l1_scale_probs(b, 0)
            l1_scale_probs(b, 1)
            l1_root(b)


def kernel(x, adj, L0_gnn_W_left, L0_gnn_W_right, L0_gnn_W_lin, L0_gnn_b_lin, L0_gnn_ln_a, L0_gnn_ln_b,
           L1_gnn_Wq, L1_gnn_Wk, L1_gnn_Wv, L1_gnn_bv, L1_gnn_Wo, L1_gnn_bo):
    import numpy as np
    import concourse.bacc as bacc
    from concourse import mybir as _mybir
    from concourse.bass_utils import run_bass_kernel_spmd

    x, adj = np.ascontiguousarray(x), np.ascontiguousarray(adj)
    H = x.shape[-1]
    HC = H // 128
    wl, wr, wn = (np.asarray(w) for w in (L0_gnn_W_left, L0_gnn_W_right, L0_gnn_W_lin))
    mats = [wl[0], wr[0], wn[0], wl[1], wr[1], wn[1]]
    mats += [np.asarray(w) for w in (L1_gnn_Wq, L1_gnn_Wk, L1_gnn_Wv, L1_gnn_Wo)]
    stacked = np.stack(mats).transpose(2, 0, 1).reshape(HC, 128, len(mats), H)
    weights = np.ascontiguousarray(stacked.transpose(1, 2, 0, 3)).reshape(128, len(mats), HC * H)
    b_lin, ln_a, ln_b = (np.asarray(t) for t in (L0_gnn_b_lin, L0_gnn_ln_a, L0_gnn_ln_b))
    rows = np.ascontiguousarray(np.stack([b_lin[0], b_lin[1], ln_a[1], ln_b[1],
                                          np.asarray(L1_gnn_bv), np.asarray(L1_gnn_bo)]))
    cols = np.ascontiguousarray(np.stack([ln_a[0], ln_b[0]]).reshape(2, HC, 128).transpose(2, 0, 1))

    nc = bacc.Bacc("TRN2", target_bir_lowering=False, num_devices=1)
    arrays = {"x_dram": x, "adj_dram": adj, "weights_dram": weights, "rows_dram": rows, "cols_dram": cols}
    args = [nc.dram_tensor(name, a.shape, _mybir.dt.from_np(a.dtype), kind="ExternalInput").ap()
            for name, a in arrays.items()]
    out = nc.dram_tensor("out_dram", x.shape, _mybir.dt.from_np(x.dtype), kind="ExternalOutput").ap()
    graph_net_kernel(nc, *args, out)
    return run_bass_kernel_spmd(nc, [arrays], core_ids=[0]).results[0]["out_dram"]
```

```python
from contextlib import ExitStack

import concourse.bass as bass
from concourse import mybir
from concourse.alu_op_type import AluOpType as ALU

ACT = mybir.ActivationFunctionType
F32 = mybir.dt.float32
F16 = mybir.dt.float16
AX = mybir.AxisListType.X

P = 128
BU = 2
COLS = BU * P
HEADS = 12
GROUPS = 4
W_SCALE = 64.0

LEFT, RIGHT, LIN = (0, 3), (1, 4), (2, 5)
WQ, WK, WV, WO = 6, 7, 8, 9
MATS = 10
B_LIN, LN_A1, LN_B1, BV, BO = (0, 1), 2, 3, 4, 5
ROWS = 6


class Unit:

    def __init__(self, n, half, parity):
        self.n, self.half, self.parity = n, half, parity

    @property
    def first(self):
        return isinstance(self.n, int) and self.n == 0


def even(k):
    return Unit(2 * k, k, 0)


def odd(k):
    return Unit(2 * k + 1, k, 1)


def following(unit):
    return even(unit.half + 1) if unit.parity else odd(unit.half)


class Steps:

    def __init__(self, sem, names):
        self.sem, self.names = sem, names

    def at(self, unit, name, back=0):
        return (unit.n - back) * len(self.names) + self.names.index(name) + 1


class Banks:

    def __init__(self, uses, by_act, by_dve, filled, act_took, dve_took):
        self.banks, uses = uses, list(uses)
        self.uses = uses
        self.filled = Steps(filled, uses)
        self.act_took = Steps(act_took, [u for u in uses if by_act(u)])
        self.dve_took = Steps(dve_took, [u for u in uses if by_dve(u)])
        self.readers = [self.act_took, self.dve_took]

    def bank(self, use):
        return self.banks[use]

    def before(self, use):
        same = [other for other in self.uses if self.banks[other] == self.banks[use]]
        k = same.index(use)
        return same[k - 1], int(k == 0)


def graph_net_kernel(nc, x, adj, weights, rows, cols, out):
    N, S, H = x.shape
    assert S == P and H % P == 0
    HC = H // P
    D = H // HEADS
    UNITS = N // BU
    LOOPS = (UNITS - 2) // 2
    assert UNITS == 2 * LOOPS + 2 and HC * GROUPS == HEADS and D * GROUPS == P
    TEMPER = float(H) ** 0.5
    SCALE = float(H) ** -0.5
    UNBIAS = (H / (H - 1.0)) ** 0.5

    x_u = x.rearrange("(u b) s h -> u s b h", b=BU)
    adj_u = adj.rearrange("(u b) s t -> u s b t", b=BU)
    out_u = out.rearrange("(u b) s h -> u s b h", b=BU)

    with ExitStack() as ctx:
        def sb(name, shape, dt=F32):
            return ctx.enter_context(nc.sbuf_tensor(name, shape, dt))

        def sem(name):
            return ctx.enter_context(nc.semaphore(name))

        psum = ctx.enter_context(nc.psum_tensor("psum", [P, 8, 512], F32))

        ident = sb("ident", [P, P])
        tri_left = sb("tri_left", [P, P])
        tri_right = sb("tri_right", [P, P])
        half_power = sb("half_power", [P, BU])
        minus_half_power = sb("minus_half_power", [P, BU])
        stage = sb("stage", [P, 3, HC * H])
        w_hi = sb("w_hi", [P, MATS, HC, H], F16)
        w_lo = sb("w_lo", [P, MATS, HC, H], F16)
        row = sb("row", [P, ROWS, H])
        ln_col = sb("ln_col", [P, 2, HC])

        x_nat = sb("x_nat", [P, 2, BU, H])
        adj_nat = sb("adj_nat", [P, 2, BU, P])
        hT_hi = sb("hT_hi", [P, HC, COLS], F16)
        hT_lo = sb("hT_lo", [P, HC, COLS], F16)
        adjT = sb("adjT", [P, BU, P])
        side_mask = sb("side_mask", [P, BU, 2, P])
        m_hi = sb("m_hi", [P, HC, 2, COLS], F16)
        m_lo = sb("m_lo", [P, HC, 2, COLS], F16)
        lin = sb("lin", [P, BU, H + 1])
        masked = sb("masked", [P, BU, 2, P])
        scoreT = sb("scoreT", [P, BU, P])
        expT = sb("expT", [P, BU, P])
        attT = sb("attT", [P, BU, P])
        z = sb("z", [P, BU, H])
        h_T = sb("h_T", [P, HC, COLS])
        scaled = sb("scaled", [P, BU, H])
        shifted = sb("shifted", [P, BU, H])
        y = sb("y", [P, BU, H])
        stats = sb("stats", [P, BU, 6])
        moments = sb("moments", [P, BU, 2])
        pause = sb("pause", [P, 1])
        eps_term = sb("eps_term", [P, BU])
        root = sb("root", [P, BU])
        spread = sb("spread", [P, BU])
        ln_scale = sb("ln_scale", [P, BU])
        ln_shift = sb("ln_shift", [P, BU])

        x1 = sb("x1", [P, BU, H])
        residual = sb("residual", [P, BU, H])
        xT_hi = sb("xT_hi", [P, HC, COLS], F16)
        xT_lo = sb("xT_lo", [P, HC, COLS], F16)
        qk_hi = sb("qk_hi", [P, HC, 2, COLS], F16)
        qk_lo = sb("qk_lo", [P, HC, 2, COLS], F16)
        v = sb("v", [P, BU, H])
        probs = sb("probs", [P, BU, HEADS, P])
        probsT = sb("probsT", [P, BU, HEADS, P])
        minus_max = sb("minus_max", [P, BU, HEADS])
        minimum = sb("minimum", [P, BU, HEADS])
        max_nonzero = sb("max_nonzero", [P, BU, HEADS])
        live = sb("live", [P, BU, HEADS])
        prob_sum = sb("prob_sum", [P, BU, HEADS])
        inverse_sum = sb("inverse_sum", [P, BU, HEADS])
        prob_scale = sb("prob_scale", [P, BU, HEADS])
        oT_hi = sb("oT_hi", [P, BU, HC, P], F16)
        oT_lo = sb("oT_lo", [P, BU, HC, P], F16)
        y2 = sb("y2", [P, BU, H])
        stats2 = sb("stats2", [P, BU, 6])
        moments2 = sb("moments2", [P, BU, 2])
        variance2 = sb("variance2", [P, BU])
        root2 = sb("root2", [P, BU])
        ln_shift2 = sb("ln_shift2", [P, BU])
        result = sb("result", [P, BU, H])

        x_loaded = [sem(f"x_loaded{p}") for p in range(2)]
        adj_loaded = [sem(f"adj_loaded{p}") for p in range(2)]
        weight_loaded = [sem(f"weight_loaded{k}") for k in range(3)]
        rows_loaded = sem("rows_loaded")
        weight_hi_ready = sem("weight_hi_ready")
        weight_ready = sem("weight_ready")
        const_set = sem("const_set")
        consts_ready = sem("consts_ready")
        rows_ready = sem("rows_ready")

        layer_banks = (("m{}_0", 0), ("m{}_1", 1), ("m{}_2", 2), ("lin{}_0", 3), ("u{}", 0), ("lin{}_1", 1),
                       ("ctx{}_0", 2), ("ctx{}_1", 3))
        l0 = Banks(
            {"xT0": 0, "xT1": 1, **{use.format(0): bank for use, bank in layer_banks},
             "hT0": 0, "hT1": 1, **{use.format(1): bank for use, bank in layer_banks}},
            lambda u: u[0] in "xmh",
            lambda u: u[0] in "xmluc",
            sem("l0_filled"), sem("l0_act_took"), sem("l0_dve_took"))
        normed = Steps(sem("normed"), ["ctx0_0", "ctx0_1", "ctx1_0", "ctx1_1"])
        l0.readers.append(normed)
        masks_ready = Steps(sem("masks_ready"), ["masks"])
        scores_ready = Steps(sem("scores_ready"), ["layer0", "layer1"])
        exp_ready = Steps(sem("exp_ready"), ["layer0", "layer1"])
        att_ready = Steps(sem("att_ready"), ["layer0", "layer1"])
        var_ready = Steps(sem("var_ready"), ["layer0", "layer1", "x1"])
        root_ready = Steps(sem("root_ready"), ["layer0", "layer1", "x1"])
        coef_ready = Steps(sem("coef_ready"), ["layer0", "layer1", "x1"])
        hT_ready = Steps(sem("hT_ready"), ["hi", "lo"])
        gain_ready = Steps(sem("gain_ready"), ["scaled"])
        x1_ready = Steps(sem("x1_ready"), ["x1"])
        l0_own = Steps(sem("l0_own"), [f"{s}{l}" for l in range(2) for s in ("stats", "spread", "scale")]
                       + ["shifted", "y", "ystats", "ymoments"])

        l1_uses = ["xT0", "xT1", "qk0", "qk1", "qk2"] \
            + [use for b in range(BU) for use in [f"s{b}_{g}" for g in range(GROUPS)] + [f"v{b}"]] + [f"pT{b}_{c}" for b in range(BU) for c in range(HC)] + ["oT0", "oT1", "y0", "y1"]
        l1 = Banks(
            {use: 4 + k % 4 for k, use in enumerate(l1_uses)},
            lambda u: u[0] in "xqpo",
            lambda u: u[0] in "xqsvoy",
            sem("l1_filled"), sem("l1_act_took"), sem("l1_dve_took"))
        residual_ready = Steps(sem("residual_ready"), ["residual"])
        extrema_ready = Steps(sem("extrema_ready"), ["graph0", "graph1"])
        probs_ready = Steps(sem("probs_ready"), ["graph0", "graph1"])
        prob_scale_ready = Steps(sem("prob_scale_ready"), ["graph0", "graph1"])
        probs_scaled = [Steps(sem(f"probs_scaled{b}"), [f"graph{b}"]) for b in range(BU)]
        var2_ready = Steps(sem("var2_ready"), ["y2"])
        root2_ready = Steps(sem("root2_ready"), ["y2"])
        coef2_ready = Steps(sem("coef2_ready"), ["y2"])
        result_ready = Steps(sem("result_ready"), ["result"])
        result_stored = sem("result_stored")
        l1_own = Steps(sem("l1_own"), ["nonzero0", "live0", "nonzero1", "live1", "inverse0", "inverse1",
                                       "stats2", "moments2"])

        def loads(unit):
            return 16 * unit.half + 16

        def bank0(use, a=0, b=512):
            return psum[:, l0.bank(use), a:b]

        def bank1(use, a=0, b=512):
            return psum[:, l1.bank(use), a:b]

        block = ctx.enter_context(nc.Block())

        @block.sync
        def _(sp):
            def load_x(p, n):
                sp.dma_start(x_nat[:, p, :, :], x_u[n]).then_inc(x_loaded[p], 16)

            def load_adj(p, n):
                sp.dma_start(adj_nat[:, p, :, :], adj_u[n]).then_inc(adj_loaded[p], 16)

            def store(c):
                sp.wait_ge(result_ready.sem, result_ready.at(c, "result"))
                sp.dma_start(out_u[c.n], result[:, :, :]).then_inc(result_stored, 16)

            def phase(a, b, c):
                sp.wait_ge(coef_ready.sem, coef_ready.at(b, "x1"))
                load_x(1 - a.parity, a.n + 1)
                if c is not None:
                    store(c)
                sp.wait_ge(l1.dve_took.sem, l1.dve_took.at(b, "s1_3"))
                load_adj(1 - a.parity, a.n + 1)

            load_x(0, 0)
            load_adj(0, 0)
            for w in range(MATS):
                if w >= 3:
                    sp.wait_ge(weight_ready, w - 2)
                sp.dma_start(stage[:, w % 3, :], weights[:, w]).then_inc(weight_loaded[w % 3], 16)
                if w == 1:
                    sp.dma_start(row[:, :, :], rows.partition_broadcast(P)).then_inc(rows_loaded, 16)
                    sp.dma_start(ln_col[:, :, :], cols).then_inc(rows_loaded, 16)
                if w == 2:
                    load_x(1, 1)
                    load_adj(1, 1)
            phase(odd(0), even(0), None)
            with sp.Fori(0, LOOPS - 1) as i:
                phase(even(i + 1), odd(i), even(i))
                phase(odd(i + 1), even(i + 1), odd(i))
            phase(even(LOOPS), odd(LOOPS - 1), even(LOOPS - 1))
            for c in (odd(LOOPS - 1), even(LOOPS), odd(LOOPS)):
                store(c)
            sp.wait_ge(result_stored, 16 * UNITS)

        @block.tensor
        def _(pe):
            def bank_free(banks, unit, use):
                old, back = banks.before(use)
                if back and unit.first:
                    return
                for took in banks.readers:
                    if old in took.names:
                        pe.wait_ge(took.sem, took.at(unit, old, back))

            def split_product(o, lhs, rhs, terms):
                last = None
                for t in range(terms):
                    for n, (lh, rh) in enumerate(((0, 0), (0, 1), (1, 0))):
                        last = pe.matmul(o, lhs(lh, t), rhs(rh, t), start=(t == 0 and n == 0),
                                         stop=(t == terms - 1 and n == 2))
                return last

            w_half, hT_half, m_half = (w_hi, w_lo), (hT_hi, hT_lo), (m_hi, m_lo)
            xT_half, qk_half, oT_half = (xT_hi, xT_lo), (qk_hi, qk_lo), (oT_hi, oT_lo)

            def transpose_rows(banks, unit, uses, source, extra=None):
                for k, use in enumerate(uses):
                    bank_free(banks, unit, use)
                    o = psum[:, banks.bank(use), :].rearrange("p (c b n) -> p c b n", c=2, b=BU)
                    for c in range(2 * k, min(2 * k + 2, HC)):
                        for b in range(BU):
                            last = pe.transpose(o[:, c % 2, b, :], source[:, b, c * P:(c + 1) * P], ident[:, :])
                    if k == 1 and extra is not None:
                        for b in range(BU):
                            last = pe.transpose(o[:, 1, b, :], extra[:, b, :], ident[:, :])
                    last.then_inc(banks.filled.sem, 1)

            def l0_xT(u):
                pe.wait_ge(x_loaded[u.parity], loads(u))
                pe.wait_ge(adj_loaded[u.parity], loads(u))
                transpose_rows(l0, u, ("xT0", "xT1"), x_nat[:, u.parity], adj_nat[:, u.parity])

            def l0_m(u, l, c):
                if c == 0 and l == 0:
                    pe.wait_ge(l0.act_took.sem, l0.act_took.at(u, "xT1"))
                    pe.wait_ge(l0.dve_took.sem, l0.dve_took.at(u, "xT1"))
                if c == 0 and l == 1:
                    pe.wait_ge(hT_ready.sem, hT_ready.at(u, "lo"))
                use = f"m{l}_{c}"
                bank_free(l0, u, use)
                for side, mat in enumerate((LEFT[l], RIGHT[l])):
                    last = split_product(bank0(use, side * COLS, (side + 1) * COLS),
                                         lambda h, t: w_half[h][:, mat, t, c * P:(c + 1) * P],
                                         lambda h, t: hT_half[h][:, t, :], HC)
                last.then_inc(l0.filled.sem, 1)

            def l0_lin(u, l, b):
                use = f"lin{l}_{b}"
                bank_free(l0, u, use)
                split_product(bank0(use, 0, H), lambda h, t: hT_half[h][:, t, b * P:(b + 1) * P],
                              lambda h, t: w_half[h][:, LIN[l], t, :], HC).then_inc(l0.filled.sem, 1)

            def l0_u(u, l):
                use = f"u{l}"
                pe.wait_ge(l0.act_took.sem, l0.act_took.at(u, f"m{l}_2"))
                pe.wait_ge(l0.dve_took.sem, l0.dve_took.at(u, f"m{l}_2"))
                bank_free(l0, u, use)
                for b in range(BU):
                    for side in range(2):
                        k = 2 * b + side
                        last = split_product(bank0(use, k * P, (k + 1) * P),
                                             lambda h, t: m_half[h][:, t, side, b * P:(b + 1) * P],
                                             lambda h, t: hT_half[h][:, t, b * P:(b + 1) * P], HC)
                last.then_inc(l0.filled.sem, 1)

            def l0_ctx(u, l):
                pe.wait_ge(att_ready.sem, att_ready.at(u, f"layer{l}"))
                pe.wait_ge(l0.dve_took.sem, l0.dve_took.at(u, f"lin{l}_1"))
                for b in range(BU):
                    use = f"ctx{l}_{b}"
                    bank_free(l0, u, use)
                    pe.matmul(bank0(use, 0, H + 1), attT[:, b, :], lin[:, b, :], start=True,
                              stop=True).then_inc(l0.filled.sem, 1)

            def l0_hT(u):
                pe.wait_ge(normed.sem, normed.at(u, "ctx0_1"))
                pe.wait_ge(l0.dve_took.sem, l0.dve_took.at(u, "ctx0_1"))
                transpose_rows(l0, u, ("hT0", "hT1"), z)

            def l1_xT(u):
                pe.wait_ge(x1_ready.sem, x1_ready.at(u, "x1"))
                transpose_rows(l1, u, ("xT0", "xT1"), x1)

            def l1_qk(u, c):
                if c == 0:
                    pe.wait_ge(l1.act_took.sem, l1.act_took.at(u, "xT1"))
                    pe.wait_ge(l1.dve_took.sem, l1.dve_took.at(u, "xT1"))
                use = f"qk{c}"
                bank_free(l1, u, use)
                for side, mat in enumerate((WQ, WK)):
                    last = split_product(bank1(use, side * COLS, (side + 1) * COLS),
                                         lambda h, t: w_half[h][:, mat, t, c * P:(c + 1) * P],
                                         lambda h, t: xT_half[h][:, t, :], HC)
                last.then_inc(l1.filled.sem, 1)

            def l1_s(u, b):
                if b == 0:
                    pe.wait_ge(l1.act_took.sem, l1.act_took.at(u, "qk2"))
                    pe.wait_ge(l1.dve_took.sem, l1.dve_took.at(u, "qk2"))
                for g0 in (0, 2):
                    for g in (g0, g0 + 1):
                        bank_free(l1, u, f"s{b}_{g}")
                    for c in range(HC):
                        for n, (lh, rh) in enumerate(((0, 0), (0, 1), (1, 0))):
                            for g in (g0, g0 + 1):
                                use = f"s{b}_{g}"
                                r = slice(g * D, (g + 1) * D)
                                mm = pe.matmul(bank1(use, c * P, (c + 1) * P),
                                               qk_half[lh][r, c, 0, b * P:(b + 1) * P],
                                               qk_half[rh][r, c, 1, b * P:(b + 1) * P],
                                               start=(n == 0), stop=(n == 2))
                                if c == HC - 1 and n == 2:
                                    mm.then_inc(l1.filled.sem, 1)

            def l1_v(u, b):
                use = f"v{b}"
                bank_free(l1, u, use)
                split_product(bank1(use, 0, H), lambda h, t: xT_half[h][:, t, b * P:(b + 1) * P],
                              lambda h, t: w_half[h][:, WV, t, :], HC).then_inc(l1.filled.sem, 1)

            def l1_pT(u, b):
                pe.wait_ge(probs_scaled[b].sem, probs_scaled[b].at(u, f"graph{b}"))
                for c in range(HC):
                    use = f"pT{b}_{c}"
                    bank_free(l1, u, use)
                    for k in range(4):
                        last = pe.transpose(bank1(use, k * P, (k + 1) * P), probs[:, b, 4 * c + k, :], ident[:, :])
                    last.then_inc(l1.filled.sem, 1)

            def l1_oT(u, b):
                use = f"oT{b}"
                pe.wait_ge(l1.act_took.sem, l1.act_took.at(u, f"pT{b}_{HC - 1}"))
                if b == 0:
                    pe.wait_ge(l1.dve_took.sem, l1.dve_took.at(u, "v1"))
                bank_free(l1, u, use)
                for c in range(HC):
                    for g in range(GROUPS):
                        head = c * GROUPS + g
                        last = pe.matmul(psum[g * D:(g + 1) * D, l1.bank(use), c * P:(c + 1) * P],
                                         v[:, b, head * D:(head + 1) * D], probsT[:, b, g * HC + c, :],
                                         start=True, stop=True)
                last.then_inc(l1.filled.sem, 1)

            def l1_y(u, b):
                use = f"y{b}"
                pe.wait_ge(l1.act_took.sem, l1.act_took.at(u, f"oT{b}"))
                pe.wait_ge(l1.dve_took.sem, l1.dve_took.at(u, f"oT{b}"))
                bank_free(l1, u, use)
                split_product(bank1(use, 0, H), lambda h, t: oT_half[h][:, b, t, :],
                              lambda h, t: w_half[h][:, WO, t, :], HC).then_inc(l1.filled.sem, 1)

            def phase(a, b, c, more=True):
                if c is not None:
                    l1_pT(c, 0)
                l0_m(a, 0, 0)
                if c is not None:
                    l1_pT(c, 1)
                l0_m(a, 0, 1)
                if c is not None:
                    l1_oT(c, 0)
                l0_m(a, 0, 2)
                if c is not None:
                    l1_oT(c, 1)
                l0_lin(a, 0, 0)
                if c is not None:
                    l1_y(c, 0)
                    l1_y(c, 1)
                l1_xT(b)
                l0_u(a, 0)
                l0_lin(a, 0, 1)
                l1_qk(b, 0)
                l0_ctx(a, 0)
                l1_qk(b, 1)
                l1_qk(b, 2)
                l0_hT(a)
                l1_s(b, 0)
                l1_v(b, 0)
                l0_m(a, 1, 0)
                l1_s(b, 1)
                l0_m(a, 1, 1)
                l0_m(a, 1, 2)
                l0_lin(a, 1, 0)
                l0_u(a, 1)
                l0_lin(a, 1, 1)
                l1_v(b, 1)
                l0_ctx(a, 1)
                if more:
                    l0_xT(following(a))

            def l1_end(c):
                l1_pT(c, 0)
                l1_pT(c, 1)
                l1_oT(c, 0)
                l1_oT(c, 1)
                l1_y(c, 0)
                l1_y(c, 1)

            pe.wait_ge(consts_ready, 1)
            a = even(0)
            l0_xT(a)
            for l in range(2):
                pe.wait_ge(weight_ready, LIN[l])
                for c in range(HC):
                    l0_m(a, l, c)
                pe.wait_ge(weight_ready, LIN[l] + 1)
                l0_lin(a, l, 0)
                l0_u(a, l)
                l0_lin(a, l, 1)
                l0_ctx(a, l)
                if l == 0:
                    l0_hT(a)
            l0_xT(odd(0))
            pe.wait_ge(weight_ready, MATS)
            phase(odd(0), even(0), None)
            with pe.Fori(0, LOOPS - 1) as i:
                phase(even(i + 1), odd(i), even(i))
                phase(odd(i + 1), even(i + 1), odd(i))
            phase(even(LOOPS), odd(LOOPS - 1), even(LOOPS - 1))
            phase(odd(LOOPS), even(LOOPS), odd(LOOPS - 1), more=False)
            l1_end(even(LOOPS))
            b = odd(LOOPS)
            l1_xT(b)
            for c in range(HC):
                l1_qk(b, c)
            for g in range(BU):
                l1_s(b, g)
                l1_v(b, g)
            l1_end(b)

        @block.scalar
        def _(act):
            def flat(t, k, n):
                return t[:, 2 * k:2 * k + n, :].rearrange("p c n -> p (c n)")

            def weight_high(w):
                act.wait_ge(weight_loaded[w % 3], 16 * (w // 3) + 16)
                act.activation(w_hi[:, w].rearrange("p c n -> p (c n)"), stage[:, w % 3, :], ACT.Copy,
                               scale=W_SCALE).then_inc(weight_hi_ready, 1)

            def l0_xT(u):
                act.wait_ge(l0.filled.sem, l0.filled.at(u, "xT0"))
                act.activation(flat(hT_hi, 0, 2), bank0("xT0"), ACT.Copy).then_inc(l0.act_took.sem, 1)
                act.wait_ge(l0.filled.sem, l0.filled.at(u, "xT1"))
                act.activation(flat(hT_hi, 1, 1), bank0("xT1", 0, COLS), ACT.Copy)
                act.activation(adjT[:, :, :].rearrange("p b n -> p (b n)"), bank0("xT1", COLS), ACT.Copy)\
                   .then_inc(l0.act_took.sem, 1)

            def l0_m(u, l, c):
                act.wait_ge(l0.filled.sem, l0.filled.at(u, f"m{l}_{c}"))
                act.activation(m_hi[:, c].rearrange("p s n -> p (s n)"), bank0(f"m{l}_{c}"), ACT.Copy)\
                   .then_inc(l0.act_took.sem, 1)

            def l0_exp(u, l):
                act.wait_ge(scores_ready.sem, scores_ready.at(u, f"layer{l}"))
                act.activation(expT[:, :, :], scoreT[:, :, :], ACT.Exp, scale=1.0 / (W_SCALE * TEMPER))\
                   .then_inc(exp_ready.sem, 1)

            def l0_norm(u, l):
                act.wait_ge(coef_ready.sem, coef_ready.at(u, f"layer{l}"))
                for b in range(BU):
                    act.activation(z[:, b, :], bank0(f"ctx{l}_{b}", 0, H), ACT.Identity,
                                   bias=ln_shift[:, b:b + 1], scale=ln_scale[:, b:b + 1])\
                       .then_inc(normed.sem, 1)

            def l0_hT(u):
                for k, use in enumerate(("hT0", "hT1")):
                    act.wait_ge(l0.filled.sem, l0.filled.at(u, use))
                    for c in range(2 * k, min(2 * k + 2, HC)):
                        last = act.activation(h_T[:, c, :], bank0(use, c % 2 * COLS, (c % 2 + 1) * COLS), ACT.Relu,
                                              bias=ln_col[:, 1, c:c + 1], scale=ln_col[:, 0, c:c + 1])
                    last.then_inc(l0.act_took.sem, 1)

            def l0_x1(u):
                act.wait_ge(coef_ready.sem, coef_ready.at(u, "x1"))
                for b in range(BU):
                    last = act.activation(x1[:, b, :], y[:, b, :], ACT.Identity,
                                          bias=ln_shift[:, b:b + 1], scale=ln_scale[:, b:b + 1])
                last.then_inc(x1_ready.sem, 1)

            def l1_xT(u):
                for k, use in enumerate(("xT0", "xT1")):
                    n = 2 - k
                    act.wait_ge(l1.filled.sem, l1.filled.at(u, use))
                    act.activation(flat(xT_hi, k, n), bank1(use, 0, n * COLS), ACT.Copy).then_inc(l1.act_took.sem, 1)

            def l1_qk(u, c):
                act.wait_ge(l1.filled.sem, l1.filled.at(u, f"qk{c}"))
                act.activation(qk_hi[:, c].rearrange("p s n -> p (s n)"), bank1(f"qk{c}"), ACT.Copy)\
                   .then_inc(l1.act_took.sem, 1)

            def l1_exp(u, b, part):
                if part == 0:
                    act.wait_ge(extrema_ready.sem, extrema_ready.at(u, f"graph{b}"))
                for k in range(3 * part, 3 * part + 3):
                    last = act.activation(probs[:, b, k, :], probs[:, b, k, :], ACT.Exp,
                                          bias=minus_max[:, b, k:k + 1], accum_out=prob_sum[:, b, k:k + 1])
                if part == 3:
                    last.then_inc(probs_ready.sem, 1)

            def l1_pT(u, b):
                for c in range(HC):
                    act.wait_ge(l1.filled.sem, l1.filled.at(u, f"pT{b}_{c}"))
                    act.activation(probsT[:, b, 4 * c:4 * c + 4, :].rearrange("p k n -> p (k n)"),
                                   bank1(f"pT{b}_{c}"), ACT.Copy).then_inc(l1.act_took.sem, 1)

            def l1_oT(u, b):
                act.wait_ge(l1.filled.sem, l1.filled.at(u, f"oT{b}"))
                act.activation(oT_hi[:, b].rearrange("p c n -> p (c n)"), bank1(f"oT{b}", 0, H), ACT.Copy)\
                   .then_inc(l1.act_took.sem, 1)

            def l1_result(u):
                act.wait_ge(coef2_ready.sem, coef2_ready.at(u, "y2"))
                if not u.first:
                    act.wait_ge(result_stored, 16 * u.n)
                for b in range(BU):
                    last = act.activation(result[:, b, :], y2[:, b, :], ACT.Identity,
                                          bias=ln_shift2[:, b:b + 1], scale=root2[:, b:b + 1])
                last.then_inc(result_ready.sem, 1)

            def phase(a, b, c, more=True):
                if c is not None:
                    l1_pT(c, 0)
                l0_norm(b, 1)
                l0_m(a, 0, 0)
                if c is not None:
                    l1_pT(c, 1)
                l0_m(a, 0, 1)
                if c is not None:
                    l1_oT(c, 0)
                l0_m(a, 0, 2)
                if c is not None:
                    l1_oT(c, 1)
                l0_x1(b)
                l1_xT(b)
                l0_exp(a, 0)
                l1_qk(b, 0)
                if c is not None:
                    l1_result(c)
                l1_qk(b, 1)
                l0_norm(a, 0)
                l1_qk(b, 2)
                l0_hT(a)
                l0_m(a, 1, 0)
                l1_exp(b, 0, 0)
                l0_m(a, 1, 1)
                l1_exp(b, 0, 1)
                l1_exp(b, 0, 2)
                l0_m(a, 1, 2)
                l1_exp(b, 0, 3)
                l1_exp(b, 1, 0)
                l1_exp(b, 1, 1)
                l0_exp(a, 1)
                l1_exp(b, 1, 2)
                l1_exp(b, 1, 3)
                if more:
                    l0_xT(following(a))

            def l1_end(c):
                l1_pT(c, 0)
                l1_pT(c, 1)
                l1_oT(c, 0)
                l1_oT(c, 1)
                l1_result(c)

            for w in range(3):
                weight_high(w)
            act.wait_ge(rows_loaded, 32)
            a = even(0)
            l0_xT(a)
            for c in range(HC):
                l0_m(a, 0, c)
            for w in range(3, 6):
                weight_high(w)
            l0_exp(a, 0)
            l0_norm(a, 0)
            l0_hT(a)
            for c in range(HC):
                l0_m(a, 1, c)
            for w in range(6, MATS):
                weight_high(w)
            l0_exp(a, 1)
            l0_xT(odd(0))
            phase(odd(0), even(0), None)
            with act.Fori(0, LOOPS - 1) as i:
                phase(even(i + 1), odd(i), even(i))
                phase(odd(i + 1), even(i + 1), odd(i))
            phase(even(LOOPS), odd(LOOPS - 1), even(LOOPS - 1))
            phase(odd(LOOPS), even(LOOPS), odd(LOOPS - 1), more=False)
            b = odd(LOOPS)
            l0_norm(b, 1)
            l1_end(even(LOOPS))
            l0_x1(b)
            l1_xT(b)
            for c in range(HC):
                l1_qk(b, c)
            for g in range(BU):
                for part in range(4):
                    l1_exp(b, g, part)
            l1_end(b)

        @block.vector
        def _(dve):
            def flat(t, k, n):
                return t[:, 2 * k:2 * k + n, :].rearrange("p c n -> p (c n)")

            def weight_low(w):
                dve.wait_ge(weight_hi_ready, w + 1)
                dve.scalar_tensor_tensor(out=w_lo[:, w].rearrange("p c n -> p (c n)"), in0=stage[:, w % 3, :],
                                         scalar=W_SCALE, in1=w_hi[:, w].rearrange("p c n -> p (c n)"),
                                         op0=ALU.mult, op1=ALU.subtract).then_inc(weight_ready, 1)

            def low_half(banks, unit, use, lo, hi, n):
                dve.wait_ge(banks.act_took.sem, banks.act_took.at(unit, use))
                dve.tensor_tensor(lo, psum[:, banks.bank(use), 0:n], hi, ALU.subtract)\
                   .then_inc(banks.dve_took.sem, 1)

            def l0_xT(u):
                for k, use in enumerate(("xT0", "xT1")):
                    low_half(l0, u, use, flat(hT_lo, k, 2 - k), flat(hT_hi, k, 2 - k), (2 - k) * COLS)

            def l0_m(u, l, c):
                low_half(l0, u, f"m{l}_{c}", m_lo[:, c].rearrange("p s n -> p (s n)"),
                         m_hi[:, c].rearrange("p s n -> p (s n)"), 2 * COLS)

            def l0_lin(u, l, b):
                dve.wait_ge(l0.filled.sem, l0.filled.at(u, f"lin{l}_{b}"))
                dve.tensor_tensor(lin[:, b, 0:H], bank0(f"lin{l}_{b}", 0, H), row[:, B_LIN[l], :], ALU.add)\
                   .then_inc(l0.dve_took.sem, 1)

            def l0_scores(u, l):
                if l == 0:
                    dve.wait_ge(masks_ready.sem, masks_ready.at(u, "masks"))
                dve.wait_ge(l0.filled.sem, l0.filled.at(u, f"u{l}"))
                dve.tensor_tensor(masked[:, :, :, :].rearrange("p b s n -> p (b s n)"), bank0(f"u{l}"),
                                  side_mask[:, :, :, :].rearrange("p b s n -> p (b s n)"), ALU.mult)\
                   .then_inc(l0.dve_took.sem, 1)
                dve.wait_ge(l0.dve_took.sem, l0.dve_took.at(u, f"u{l}"))
                dve.tensor_tensor(scoreT[:, :, :], masked[:, :, 0, :], masked[:, :, 1, :], ALU.add)\
                   .then_inc(scores_ready.sem, 1)

            def l0_att(u, l):
                dve.wait_ge(exp_ready.sem, exp_ready.at(u, f"layer{l}"))
                dve.tensor_tensor(attT[:, :, :], expT[:, :, :], adjT[:, :, :], ALU.mult).then_inc(att_ready.sem, 1)

            def l0_stats(u, l):
                for b in range(BU):
                    dve.wait_ge(l0.filled.sem, l0.filled.at(u, f"ctx{l}_{b}"))
                    last = dve.bn_stats(stats[:, b, :], bank0(f"ctx{l}_{b}", 0, H))
                    if b == BU - 1:
                        last.then_inc(l0_own.sem, 1)
                    dve.tensor_scalar(eps_term[:, b:b + 1], bank0(f"ctx{l}_{b}", H, H + 1), 1e-3,
                                      W_SCALE * 1e-3 * 1e-10, ALU.mult, ALU.add).then_inc(l0.dve_took.sem, 1)
                moments_of(l0_own, u, f"stats{l}", stats, moments, var_ready.sem)

            def moments_of(own, u, step, source, target, done):
                dve.wait_ge(own.sem, own.at(u, step))
                dve.memset(pause[:, :], 0.0)
                for b in range(BU):
                    last = dve.bn_aggr(target[:, b, :], source[:, b, :])
                last.then_inc(done, 1)

            def l0_coef(u, l):
                dve.wait_ge(root_ready.sem, root_ready.at(u, f"layer{l}"))
                dve.wait_ge(l0.dve_took.sem, l0.dve_took.at(u, f"ctx{l}_1"))
                dve.scalar_tensor_tensor(out=spread[:, :], in0=root[:, :], scalar=UNBIAS, in1=eps_term[:, :],
                                         op0=ALU.mult, op1=ALU.add).then_inc(l0_own.sem, 1)
                dve.wait_ge(l0_own.sem, l0_own.at(u, f"spread{l}"))
                dve.reciprocal(ln_scale[:, :], spread[:, :]).then_inc(l0_own.sem, 1)
                dve.wait_ge(l0_own.sem, l0_own.at(u, f"scale{l}"))
                dve.scalar_tensor_tensor(out=ln_shift[:, :], in0=moments[:, :, 0], scalar=-1.0, in1=ln_scale[:, :],
                                         op0=ALU.mult, op1=ALU.mult).then_inc(coef_ready.sem, 1)

            def l0_hT(u):
                dve.wait_ge(l0.act_took.sem, l0.act_took.at(u, "hT1"))
                dve.tensor_copy(hT_hi[:, :, :], h_T[:, :, :]).then_inc(hT_ready.sem, 1)
                dve.wait_ge(hT_ready.sem, hT_ready.at(u, "hi"))
                dve.tensor_tensor(hT_lo[:, :, :], h_T[:, :, :], hT_hi[:, :, :], ALU.subtract)\
                   .then_inc(hT_ready.sem, 1)

            def l0_y(u):
                dve.wait_ge(gain_ready.sem, gain_ready.at(u, "scaled"))
                dve.tensor_tensor(shifted[:, :, :], scaled[:, :, :],
                                  row[:, LN_B1:LN_B1 + 1, :].to_broadcast([P, BU, H]), ALU.add)\
                   .then_inc(l0_own.sem, 1)
                dve.wait_ge(l0_own.sem, l0_own.at(u, "shifted"))
                dve.scalar_tensor_tensor(out=y[:, :, :], in0=shifted[:, :, :], scalar=0.0,
                                         in1=x_nat[:, u.parity, :, :], op0=ALU.max, op1=ALU.add)\
                   .then_inc(l0_own.sem, 1)
                dve.wait_ge(l0_own.sem, l0_own.at(u, "y"))
                for b in range(BU):
                    last = dve.bn_stats(stats[:, b, :], y[:, b, :])
                last.then_inc(l0_own.sem, 1)
                moments_of(l0_own, u, "ystats", stats, moments, l0_own.sem)
                dve.wait_ge(l0_own.sem, l0_own.at(u, "ymoments"))
                dve.tensor_scalar(spread[:, :], moments[:, :, 1], 1e-5, None, ALU.add).then_inc(var_ready.sem, 1)

            def l0_y_coef(u):
                dve.wait_ge(root_ready.sem, root_ready.at(u, "x1"))
                dve.tensor_copy(ln_scale[:, :], root[:, :])
                dve.scalar_tensor_tensor(out=ln_shift[:, :], in0=moments[:, :, 0], scalar=-1.0, in1=root[:, :],
                                         op0=ALU.mult, op1=ALU.mult).then_inc(coef_ready.sem, 1)

            def l1_xT(u):
                for k, use in enumerate(("xT0", "xT1")):
                    low_half(l1, u, use, flat(xT_lo, k, 2 - k), flat(xT_hi, k, 2 - k), (2 - k) * COLS)

            def l1_qk(u, c):
                low_half(l1, u, f"qk{c}", qk_lo[:, c].rearrange("p s n -> p (s n)"),
                         qk_hi[:, c].rearrange("p s n -> p (s n)"), 2 * COLS)

            def l1_scores(u, b):
                if b == 0:
                    dve.wait_ge(adj_loaded[u.parity], loads(u))
                bias = adj_nat[:, u.parity, b, :].unsqueeze(1).to_broadcast([P, HC, P])
                for g in range(GROUPS):
                    use = f"s{b}_{g}"
                    dve.wait_ge(l1.filled.sem, l1.filled.at(u, use))
                    dve.scalar_tensor_tensor(out=probs[:, b, g * HC:(g + 1) * HC, :],
                                             in0=bank1(use, 0, H).rearrange("p (c n) -> p c n", c=HC),
                                             scalar=SCALE / (W_SCALE * W_SCALE), in1=bias,
                                             op0=ALU.mult, op1=ALU.add).then_inc(l1.dve_took.sem, 1)

            def l1_scale_probs(u, b):
                dve.wait_ge(prob_scale_ready.sem, prob_scale_ready.at(u, f"graph{b}"))
                dve.tensor_tensor(probs[:, b, :, :], probs[:, b, :, :],
                                  prob_scale[:, b, :].unsqueeze(2).to_broadcast([P, HEADS, P]), ALU.mult)\
                   .then_inc(probs_scaled[b].sem, 1)

            def l1_extrema(u, b):
                dve.wait_ge(l1.dve_took.sem, l1.dve_took.at(u, f"s{b}_3"))
                dve.tensor_reduce(minus_max[:, b, :], probs[:, b, :, :], AX, ALU.max, negate=True)
                dve.tensor_reduce(minimum[:, b, :], probs[:, b, :, :], AX, ALU.min)\
                   .then_inc(extrema_ready.sem, 1)
                dve.wait_ge(extrema_ready.sem, extrema_ready.at(u, f"graph{b}"))
                dve.tensor_scalar(max_nonzero[:, b, :], minus_max[:, b, :], 0.0, None, ALU.not_equal)\
                   .then_inc(l1_own.sem, 1)
                dve.wait_ge(l1_own.sem, l1_own.at(u, f"nonzero{b}"))
                dve.scalar_tensor_tensor(out=live[:, b, :], in0=minimum[:, b, :], scalar=0.0,
                                         in1=max_nonzero[:, b, :], op0=ALU.not_equal, op1=ALU.max)\
                   .then_inc(l1_own.sem, 1)

            def l1_prob_scale(u, b):
                dve.wait_ge(probs_ready.sem, probs_ready.at(u, f"graph{b}"))
                dve.reciprocal(inverse_sum[:, b, :], prob_sum[:, b, :]).then_inc(l1_own.sem, 1)
                dve.wait_ge(l1_own.sem, l1_own.at(u, f"inverse{b}"))
                dve.scalar_tensor_tensor(out=prob_scale[:, b, :], in0=live[:, b, :], scalar=1.0 / W_SCALE,
                                         in1=inverse_sum[:, b, :], op0=ALU.mult, op1=ALU.mult)\
                   .then_inc(prob_scale_ready.sem, 1)

            def l1_v(u, b):
                dve.wait_ge(l1.filled.sem, l1.filled.at(u, f"v{b}"))
                dve.tensor_tensor(v[:, b, :], bank1(f"v{b}", 0, H), row[:, BV, :], ALU.add)\
                   .then_inc(l1.dve_took.sem, 1)

            def l1_oT(u, b):
                low_half(l1, u, f"oT{b}", oT_lo[:, b].rearrange("p c n -> p (c n)"),
                         oT_hi[:, b].rearrange("p c n -> p (c n)"), H)

            def l1_y(u, b):
                if b == 0:
                    dve.wait_ge(residual_ready.sem, residual_ready.at(u, "residual"))
                dve.wait_ge(l1.filled.sem, l1.filled.at(u, f"y{b}"))
                dve.scalar_tensor_tensor(out=y2[:, b, :], in0=bank1(f"y{b}", 0, H), scalar=1.0 / W_SCALE,
                                         in1=residual[:, b, :], op0=ALU.mult, op1=ALU.add)\
                   .then_inc(l1.dve_took.sem, 1)

            def l1_stats(u):
                dve.wait_ge(l1.dve_took.sem, l1.dve_took.at(u, "y1"))
                for b in range(BU):
                    last = dve.bn_stats(stats2[:, b, :], y2[:, b, :])
                last.then_inc(l1_own.sem, 1)
                moments_of(l1_own, u, "stats2", stats2, moments2, l1_own.sem)
                dve.wait_ge(l1_own.sem, l1_own.at(u, "moments2"))
                dve.tensor_scalar(variance2[:, :], moments2[:, :, 1], 1e-5, None, ALU.add)\
                   .then_inc(var2_ready.sem, 1)

            def l1_coef(u):
                dve.wait_ge(root2_ready.sem, root2_ready.at(u, "y2"))
                dve.scalar_tensor_tensor(out=ln_shift2[:, :], in0=moments2[:, :, 0], scalar=-1.0, in1=root2[:, :],
                                         op0=ALU.mult, op1=ALU.mult).then_inc(coef2_ready.sem, 1)

            def phase(a, b, c, more=True):
                l0_m(a, 0, 0)
                l0_y(b)
                l0_m(a, 0, 1)
                l0_y_coef(b)
                if c is not None:
                    l1_oT(c, 0)
                l0_m(a, 0, 2)
                if c is not None:
                    l1_oT(c, 1)
                l0_lin(a, 0, 0)
                if c is not None:
                    l1_y(c, 0)
                    l1_y(c, 1)
                    l1_stats(c)
                l1_xT(b)
                l0_scores(a, 0)
                if c is not None:
                    l1_coef(c)
                l0_att(a, 0)
                l0_lin(a, 0, 1)
                l1_qk(b, 0)
                l0_stats(a, 0)
                l0_coef(a, 0)
                l1_qk(b, 1)
                l1_qk(b, 2)
                l0_hT(a)
                l1_scores(b, 0)
                l1_extrema(b, 0)
                l1_v(b, 0)
                l0_m(a, 1, 0)
                l1_scores(b, 1)
                l1_extrema(b, 1)
                l0_m(a, 1, 1)
                l0_m(a, 1, 2)
                l0_lin(a, 1, 0)
                l1_prob_scale(b, 0)
                l0_scores(a, 1)
                l0_lin(a, 1, 1)
                l0_att(a, 1)
                l1_v(b, 1)
                l0_stats(a, 1)
                if more:
                    l0_xT(following(a))
                l1_prob_scale(b, 1)
                l0_coef(a, 1)
                l1_scale_probs(b, 1)

            def l1_end(c):
                l1_oT(c, 0)
                l1_oT(c, 1)
                l1_y(c, 0)
                l1_y(c, 1)
                l1_stats(c)
                l1_coef(c)

            dve.memset(lin[:, :, H:H + 1], W_SCALE)
            for w in range(3):
                weight_low(w)
            dve.wait_ge(rows_loaded, 32)
            for r in (*B_LIN, BV):
                last = dve.tensor_scalar(row[:, r, :], row[:, r, :], W_SCALE, None, ALU.mult)
            last.then_inc(rows_ready, 1)
            dve.wait_ge(rows_ready, 1)
            a = even(0)
            l0_xT(a)
            for c in range(HC):
                l0_m(a, 0, c)
            for w in range(3, 6):
                weight_low(w)
            for l in range(2):
                if l == 1:
                    l0_coef(a, 0)
                    l0_hT(a)
                    for c in range(HC):
                        l0_m(a, 1, c)
                    for w in range(6, MATS):
                        weight_low(w)
                l0_lin(a, l, 0)
                l0_scores(a, l)
                l0_lin(a, l, 1)
                l0_att(a, l)
                l0_stats(a, l)
            l0_xT(odd(0))
            l0_coef(a, 1)
            phase(odd(0), even(0), None)
            with dve.Fori(0, LOOPS - 1) as i:
                phase(even(i + 1), odd(i), even(i))
                phase(odd(i + 1), even(i + 1), odd(i))
            phase(even(LOOPS), odd(LOOPS - 1), even(LOOPS - 1))
            phase(odd(LOOPS), even(LOOPS), odd(LOOPS - 1), more=False)
            b = odd(LOOPS)
            l1_end(even(LOOPS))
            l0_y(b)
            l0_y_coef(b)
            l1_xT(b)
            for c in range(HC):
                l1_qk(b, c)
            for g in range(BU):
                l1_scores(b, g)
                l1_extrema(b, g)
                l1_v(b, g)
            l1_prob_scale(b, 0)
            l1_prob_scale(b, 1)
            l1_scale_probs(b, 1)
            l1_end(b)

        @block.gpsimd
        def _(pool):
            def l0_masks(u):
                pool.wait_ge(l0.act_took.sem, l0.act_took.at(u, "xT1"))
                pool.tensor_tensor(side_mask[:, :, 0, :], adjT[:, :, :],
                                   tri_left[:, :].unsqueeze(1).to_broadcast([P, BU, P]), ALU.mult)
                pool.tensor_tensor(side_mask[:, :, 1, :], adj_nat[:, u.parity, :, :],
                                   tri_right[:, :].unsqueeze(1).to_broadcast([P, BU, P]), ALU.mult)\
                    .then_inc(masks_ready.sem, 1)

            def l0_root(u, l):
                pool.wait_ge(var_ready.sem, var_ready.at(u, f"layer{l}"))
                pool.tensor_tensor(root[:, :], moments[:, :, 1], half_power[:, :], ALU.pow)\
                    .then_inc(root_ready.sem, 1)

            def l0_gain(u):
                pool.wait_ge(normed.sem, normed.at(u, "ctx1_1"))
                pool.tensor_tensor(scaled[:, :, :], z[:, :, :],
                                   row[:, LN_A1:LN_A1 + 1, :].to_broadcast([P, BU, H]), ALU.mult)\
                    .then_inc(gain_ready.sem, 1)

            def l0_y_root(u):
                pool.wait_ge(var_ready.sem, var_ready.at(u, "x1"))
                pool.tensor_tensor(root[:, :], spread[:, :], minus_half_power[:, :], ALU.pow)\
                    .then_inc(root_ready.sem, 1)

            def l1_residual(u):
                pool.wait_ge(x1_ready.sem, x1_ready.at(u, "x1"))
                if not u.first:
                    pool.wait_ge(l1.dve_took.sem, l1.dve_took.at(u, "y1", back=1))
                pool.tensor_tensor(residual[:, :, :], x1[:, :, :],
                                   row[:, BO:BO + 1, :].to_broadcast([P, BU, H]), ALU.add)\
                    .then_inc(residual_ready.sem, 1)

            def l1_scale_probs(u, b):
                pool.wait_ge(prob_scale_ready.sem, prob_scale_ready.at(u, f"graph{b}"))
                pool.tensor_tensor(probs[:, b, :, :], probs[:, b, :, :],
                                   prob_scale[:, b, :].unsqueeze(2).to_broadcast([P, HEADS, P]), ALU.mult)\
                    .then_inc(probs_scaled[b].sem, 1)

            def l1_root(u):
                pool.wait_ge(var2_ready.sem, var2_ready.at(u, "y2"))
                pool.tensor_tensor(root2[:, :], variance2[:, :], minus_half_power[:, :], ALU.pow)\
                    .then_inc(root2_ready.sem, 1)

            def phase(a, b, c):
                l0_gain(b)
                l0_y_root(b)
                l0_masks(a)
                if c is not None:
                    l1_root(c)
                l1_residual(b)
                l0_root(a, 0)
                l1_scale_probs(b, 0)
                l0_root(a, 1)

            pool.memset(ident[:, :], 0.0)
            pool.memset(tri_left[:, :], 1.0)
            pool.memset(tri_right[:, :], 1.0)
            pool.memset(half_power[:, :], 0.5)
            pool.memset(minus_half_power[:, :], -0.5).then_inc(const_set, 1)
            pool.wait_ge(const_set, 1)
            pool.affine_select(out=tri_left[:, :], in_=tri_left[:, :], compare_op=ALU.is_ge, fill=0.0, base=0,
                               pattern=[[-1, P]], channel_multiplier=1)
            pool.affine_select(out=tri_right[:, :], in_=tri_right[:, :], compare_op=ALU.is_gt, fill=0.0, base=0,
                               pattern=[[1, P]], channel_multiplier=-1)
            pool.affine_select(out=ident[:, :], in_=ident[:, :], compare_op=ALU.not_equal, fill=1.0, base=0,
                               pattern=[[-1, P]], channel_multiplier=1).then_inc(consts_ready, 1)
            pool.wait_ge(consts_ready, 1)
            a = even(0)
            pool.wait_ge(rows_ready, 1)
            pool.wait_ge(adj_loaded[a.parity], loads(a))
            l0_masks(a)
            l0_root(a, 0)
            l0_root(a, 1)
            pool.wait_ge(adj_loaded[1], 16)
            phase(odd(0), even(0), None)
            with pool.Fori(0, LOOPS - 1) as i:
                phase(even(i + 1), odd(i), even(i))
                phase(odd(i + 1), even(i + 1), odd(i))
            phase(even(LOOPS), odd(LOOPS - 1), even(LOOPS - 1))
            phase(odd(LOOPS), even(LOOPS), odd(LOOPS - 1))
            b = odd(LOOPS)
            l0_gain(b)
            l1_root(even(LOOPS))
            l0_y_root(b)
            l1_residual(b)
            l1_scale_probs(b, 0)
            l1_root(b)


def kernel(x, adj, L0_gnn_W_left, L0_gnn_W_right, L0_gnn_W_lin, L0_gnn_b_lin, L0_gnn_ln_a, L0_gnn_ln_b,
           L1_gnn_Wq, L1_gnn_Wk, L1_gnn_Wv, L1_gnn_bv, L1_gnn_Wo, L1_gnn_bo):
    import numpy as np
    import concourse.bacc as bacc
    from concourse import mybir as _mybir
    from concourse.bass_utils import run_bass_kernel_spmd

    x, adj = np.ascontiguousarray(x), np.ascontiguousarray(adj)
    H = x.shape[-1]
    HC = H // 128
    wl, wr, wn = (np.asarray(w) for w in (L0_gnn_W_left, L0_gnn_W_right, L0_gnn_W_lin))
    mats = [wl[0], wr[0], wn[0], wl[1], wr[1], wn[1]]
    mats += [np.asarray(w) for w in (L1_gnn_Wq, L1_gnn_Wk, L1_gnn_Wv, L1_gnn_Wo)]
    stacked = np.stack(mats).transpose(2, 0, 1).reshape(HC, 128, len(mats), H)
    weights = np.ascontiguousarray(stacked.transpose(1, 2, 0, 3)).reshape(128, len(mats), HC * H)
    b_lin, ln_a, ln_b = (np.asarray(t) for t in (L0_gnn_b_lin, L0_gnn_ln_a, L0_gnn_ln_b))
    rows = np.ascontiguousarray(np.stack([b_lin[0], b_lin[1], ln_a[1], ln_b[1],
                                          np.asarray(L1_gnn_bv), np.asarray(L1_gnn_bo)]))
    cols = np.ascontiguousarray(np.stack([ln_a[0], ln_b[0]]).reshape(2, HC, 128).transpose(2, 0, 1))

    nc = bacc.Bacc("TRN2", target_bir_lowering=False, num_devices=1)
    arrays = {"x_dram": x, "adj_dram": adj, "weights_dram": weights, "rows_dram": rows, "cols_dram": cols}
    args = [nc.dram_tensor(name, a.shape, _mybir.dt.from_np(a.dtype), kind="ExternalInput").ap()
            for name, a in arrays.items()]
    out = nc.dram_tensor("out_dram", x.shape, _mybir.dt.from_np(x.dtype), kind="ExternalOutput").ap()
    graph_net_kernel(nc, *args, out)
    return run_bass_kernel_spmd(nc, [arrays], core_ids=[0]).results[0]["out_dram"]
```

```python
from contextlib import ExitStack

import concourse.bass as bass
from concourse import mybir
from concourse.alu_op_type import AluOpType as ALU

ACT = mybir.ActivationFunctionType
F32 = mybir.dt.float32
F16 = mybir.dt.float16
AX = mybir.AxisListType.X

P = 128
BU = 2
COLS = BU * P
HEADS = 12
GROUPS = 4
W_SCALE = 64.0

LEFT, RIGHT, LIN = (0, 3), (1, 4), (2, 5)
WQ, WK, WV, WO = 6, 7, 8, 9
MATS = 10
B_LIN, LN_A1, LN_B1, BV, BO = (0, 1), 2, 3, 4, 5
ROWS = 6


class Unit:

    def __init__(self, n, half, parity):
        self.n, self.half, self.parity = n, half, parity

    @property
    def first(self):
        return isinstance(self.n, int) and self.n == 0


def even(k):
    return Unit(2 * k, k, 0)


def odd(k):
    return Unit(2 * k + 1, k, 1)


def following(unit):
    return even(unit.half + 1) if unit.parity else odd(unit.half)


class Steps:

    def __init__(self, sem, names):
        self.sem, self.names = sem, names

    def at(self, unit, name, back=0):
        return (unit.n - back) * len(self.names) + self.names.index(name) + 1


class Banks:

    def __init__(self, uses, by_act, by_dve, filled, act_took, dve_took):
        self.banks, uses = uses, list(uses)
        self.uses = uses
        self.filled = Steps(filled, uses)
        self.act_took = Steps(act_took, [u for u in uses if by_act(u)])
        self.dve_took = Steps(dve_took, [u for u in uses if by_dve(u)])
        self.readers = [self.act_took, self.dve_took]

    def bank(self, use):
        return self.banks[use]

    def before(self, use):
        same = [other for other in self.uses if self.banks[other] == self.banks[use]]
        k = same.index(use)
        return same[k - 1], int(k == 0)


def graph_net_kernel(nc, x, adj, weights, rows, cols, out):
    N, S, H = x.shape
    assert S == P and H % P == 0
    HC = H // P
    D = H // HEADS
    UNITS = N // BU
    LOOPS = (UNITS - 2) // 2
    assert UNITS == 2 * LOOPS + 2 and HC * GROUPS == HEADS and D * GROUPS == P
    TEMPER = float(H) ** 0.5
    SCALE = float(H) ** -0.5
    UNBIAS = (H / (H - 1.0)) ** 0.5

    x_u = x.rearrange("(u b) s h -> u s b h", b=BU)
    adj_u = adj.rearrange("(u b) s t -> u s b t", b=BU)
    out_u = out.rearrange("(u b) s h -> u s b h", b=BU)

    with ExitStack() as ctx:
        def sb(name, shape, dt=F32):
            return ctx.enter_context(nc.sbuf_tensor(name, shape, dt))

        def sem(name):
            return ctx.enter_context(nc.semaphore(name))

        psum = ctx.enter_context(nc.psum_tensor("psum", [P, 8, 512], F32))

        ident = sb("ident", [P, P])
        tri_left = sb("tri_left", [P, P])
        tri_right = sb("tri_right", [P, P])
        half_power = sb("half_power", [P, BU])
        minus_half_power = sb("minus_half_power", [P, BU])
        stage = sb("stage", [P, 3, HC * H])
        w_hi = sb("w_hi", [P, MATS, HC, H], F16)
        w_lo = sb("w_lo", [P, MATS, HC, H], F16)
        row = sb("row", [P, ROWS, H])
        ln_col = sb("ln_col", [P, 2, HC])

        x_nat = sb("x_nat", [P, 2, BU, H])
        adj_nat = sb("adj_nat", [P, 2, BU, P])
        hT_hi = sb("hT_hi", [P, HC, COLS], F16)
        hT_lo = sb("hT_lo", [P, HC, COLS], F16)
        adjT = sb("adjT", [P, BU, P])
        side_mask = sb("side_mask", [P, BU, 2, P])
        m_hi = sb("m_hi", [P, HC, 2, COLS], F16)
        m_lo = sb("m_lo", [P, HC, 2, COLS], F16)
        lin = sb("lin", [P, BU, H + 1])
        masked = sb("masked", [P, BU, 2, P])
        scoreT = sb("scoreT", [P, BU, P])
        expT = sb("expT", [P, BU, P])
        attT = sb("attT", [P, BU, P])
        z = sb("z", [P, BU, H])
        h_T = sb("h_T", [P, HC, COLS])
        scaled = sb("scaled", [P, BU, H])
        shifted = sb("shifted", [P, BU, H])
        y = sb("y", [P, BU, H])
        stats = sb("stats", [P, BU, 6])
        moments = sb("moments", [P, BU, 2])
        pause = sb("pause", [P, 1])
        eps_term = sb("eps_term", [P, BU])
        root = sb("root", [P, BU])
        spread = sb("spread", [P, BU])
        ln_scale = sb("ln_scale", [P, BU])
        ln_shift = sb("ln_shift", [P, BU])

        x1 = sb("x1", [P, BU, H])
        residual = sb("residual", [P, BU, H])
        xT_hi = sb("xT_hi", [P, HC, COLS], F16)
        xT_lo = sb("xT_lo", [P, HC, COLS], F16)
        qk_hi = sb("qk_hi", [P, HC, 2, COLS], F16)
        qk_lo = sb("qk_lo", [P, HC, 2, COLS], F16)
        v = sb("v", [P, BU, H])
        scores = sb("scores", [P, BU, HEADS, P])
        probs = sb("probs", [P, BU, HEADS, P])
        probsT = sb("probsT", [P, BU, HEADS, P])
        minus_max = sb("minus_max", [P, BU, HEADS])
        minimum = sb("minimum", [P, BU, HEADS])
        max_nonzero = sb("max_nonzero", [P, BU, HEADS])
        live = sb("live", [P, BU, HEADS])
        prob_sum = sb("prob_sum", [P, BU, HEADS])
        inverse_sum = sb("inverse_sum", [P, BU, HEADS])
        prob_scale = sb("prob_scale", [P, BU, HEADS])
        oT_hi = sb("oT_hi", [P, BU, HC, P], F16)
        oT_lo = sb("oT_lo", [P, BU, HC, P], F16)
        y2 = sb("y2", [P, BU, H])
        stats2 = sb("stats2", [P, BU, 6])
        moments2 = sb("moments2", [P, BU, 2])
        variance2 = sb("variance2", [P, BU])
        root2 = sb("root2", [P, BU])
        ln_shift2 = sb("ln_shift2", [P, BU])
        result = sb("result", [P, BU, H])

        x_loaded = [sem(f"x_loaded{p}") for p in range(2)]
        adj_loaded = [sem(f"adj_loaded{p}") for p in range(2)]
        weight_loaded = [sem(f"weight_loaded{k}") for k in range(3)]
        rows_loaded = sem("rows_loaded")
        weight_hi_ready = sem("weight_hi_ready")
        weight_ready = sem("weight_ready")
        const_set = sem("const_set")
        consts_ready = sem("consts_ready")
        rows_ready = sem("rows_ready")

        layer_banks = (("m{}_0", 0), ("m{}_1", 1), ("m{}_2", 2), ("lin{}_0", 3), ("u{}", 0), ("lin{}_1", 1),
                       ("ctx{}_0", 2), ("ctx{}_1", 3))
        l0 = Banks(
            {"xT0": 0, "xT1": 1, **{use.format(0): bank for use, bank in layer_banks},
             "hT0": 0, "hT1": 1, **{use.format(1): bank for use, bank in layer_banks}},
            lambda u: u[0] in "xmh",
            lambda u: u[0] in "xmluc",
            sem("l0_filled"), sem("l0_act_took"), sem("l0_dve_took"))
        normed = Steps(sem("normed"), ["ctx0_0", "ctx0_1", "ctx1_0", "ctx1_1"])
        adjT_ready = Steps(sem("adjT_ready"), ["xT1"])
        l0.readers += [normed, adjT_ready]
        masks_ready = Steps(sem("masks_ready"), ["masks"])
        scores_ready = Steps(sem("scores_ready"), ["layer0", "layer1"])
        exp_ready = Steps(sem("exp_ready"), ["layer0", "layer1"])
        att_ready = Steps(sem("att_ready"), ["layer0", "layer1"])
        var_ready = Steps(sem("var_ready"), ["layer0", "layer1", "x1"])
        root_ready = Steps(sem("root_ready"), ["layer0", "layer1", "x1"])
        coef_ready = Steps(sem("coef_ready"), ["layer0", "layer1", "x1"])
        hT_ready = Steps(sem("hT_ready"), ["hi", "lo"])
        gain_ready = Steps(sem("gain_ready"), ["scaled"])
        x1_ready = Steps(sem("x1_ready"), ["x1"])
        l0_own = Steps(sem("l0_own"), [f"{s}{l}" for l in range(2) for s in ("stats", "spread", "scale")]
                       + ["shifted", "y", "ystats", "ymoments"])

        l1_uses = ["xT0", "xT1", "qk0", "qk1", "qk2", "v0", "s0_0", "s0_1", "s0_2", "s0_3",
                   "s1_0", "s1_1", "s1_2", "s1_3", "v1", "pT0_0", "pT0_1", "pT0_2", "oT0",
                   "pT1_0", "pT1_1", "pT1_2", "oT1", "y0", "y1"]
        in_turn = [use for use in l1_uses if use != "v0"]
        l1 = Banks(
            {use: 4 + in_turn.index(use) % 4 if use in in_turn else 3 for use in l1_uses},
            lambda u: u[0] in "xqpo",
            lambda u: u[0] in "xqsvoy",
            sem("l1_filled"), sem("l1_act_took"), sem("l1_dve_took"))
        residual_ready = Steps(sem("residual_ready"), ["residual"])
        max_ready = Steps(sem("max_ready"), ["graph0", "graph1"])
        probs_ready = Steps(sem("probs_ready"), ["graph0", "graph1"])
        prob_scale_ready = Steps(sem("prob_scale_ready"), ["graph0", "graph1"])
        probs_scaled = [Steps(sem(f"probs_scaled{b}"), [f"graph{b}"]) for b in range(BU)]
        var2_ready = Steps(sem("var2_ready"), ["y2"])
        root2_ready = Steps(sem("root2_ready"), ["y2"])
        coef2_ready = Steps(sem("coef2_ready"), ["y2"])
        result_ready = Steps(sem("result_ready"), ["result"])
        result_stored = sem("result_stored")
        l1_own = Steps(sem("l1_own"), [f"{s}{b}" for b in range(BU) for s in ("min", "nonzero", "live", "inverse")]
                       + ["stats2", "moments2"])

        def loads(unit):
            return 16 * unit.half + 16

        def bank0(use, a=0, b=512):
            return psum[:, l0.bank(use), a:b]

        def bank1(use, a=0, b=512):
            return psum[:, l1.bank(use), a:b]

        block = ctx.enter_context(nc.Block())

        @block.sync
        def _(sp):
            def load_x(p, n):
                sp.dma_start(x_nat[:, p, :, :], x_u[n]).then_inc(x_loaded[p], 16)

            def load_adj(p, n):
                sp.dma_start(adj_nat[:, p, :, :], adj_u[n]).then_inc(adj_loaded[p], 16)

            def store(c):
                sp.wait_ge(result_ready.sem, result_ready.at(c, "result"))
                sp.dma_start(out_u[c.n], result[:, :, :]).then_inc(result_stored, 16)

            def phase(a, b, c):
                sp.wait_ge(coef_ready.sem, coef_ready.at(b, "x1"))
                load_x(1 - a.parity, a.n + 1)
                if c is not None:
                    store(c)
                sp.wait_ge(l1.dve_took.sem, l1.dve_took.at(b, "s1_3"))
                load_adj(1 - a.parity, a.n + 1)

            load_x(0, 0)
            load_adj(0, 0)
            for w in range(MATS):
                if w >= 3:
                    sp.wait_ge(weight_ready, w - 2)
                sp.dma_start(stage[:, w % 3, :], weights[:, w]).then_inc(weight_loaded[w % 3], 16)
                if w == 2:
                    sp.dma_start(row[:, :, :], rows.partition_broadcast(P)).then_inc(rows_loaded, 16)
                    sp.dma_start(ln_col[:, :, :], cols).then_inc(rows_loaded, 16)
                if w == 2:
                    load_x(1, 1)
                    load_adj(1, 1)
            phase(odd(0), even(0), None)
            with sp.Fori(0, LOOPS - 1) as i:
                phase(even(i + 1), odd(i), even(i))
                phase(odd(i + 1), even(i + 1), odd(i))
            phase(even(LOOPS), odd(LOOPS - 1), even(LOOPS - 1))
            for c in (odd(LOOPS - 1), even(LOOPS), odd(LOOPS)):
                store(c)
            sp.wait_ge(result_stored, 16 * UNITS)

        @block.tensor
        def _(pe):
            def bank_free(banks, unit, use):
                old, back = banks.before(use)
                if back and unit.first:
                    return
                for took in banks.readers:
                    if old in took.names:
                        pe.wait_ge(took.sem, took.at(unit, old, back))

            def split_product(o, lhs, rhs, terms=range(HC)):
                last = None
                for t in terms:
                    for n, (lh, rh) in enumerate(((0, 0), (0, 1), (1, 0))):
                        last = pe.matmul(o, lhs(lh, t), rhs(rh, t), start=(t == 0 and n == 0),
                                         stop=(t == HC - 1 and n == 2))
                return last

            w_half, hT_half, m_half = (w_hi, w_lo), (hT_hi, hT_lo), (m_hi, m_lo)
            xT_half, qk_half, oT_half = (xT_hi, xT_lo), (qk_hi, qk_lo), (oT_hi, oT_lo)

            def transpose_rows(banks, unit, uses, source, extra=None):
                for k, use in enumerate(uses):
                    bank_free(banks, unit, use)
                    o = psum[:, banks.bank(use), :].rearrange("p (c b n) -> p c b n", c=2, b=BU)
                    for c in range(2 * k, min(2 * k + 2, HC)):
                        for b in range(BU):
                            last = pe.transpose(o[:, c % 2, b, :], source[:, b, c * P:(c + 1) * P], ident[:, :])
                    if k == 1 and extra is not None:
                        for b in range(BU):
                            last = pe.transpose(o[:, 1, b, :], extra[:, b, :], ident[:, :])
                    last.then_inc(banks.filled.sem, 1)

            def l0_xT(u):
                pe.wait_ge(x_loaded[u.parity], loads(u))
                pe.wait_ge(adj_loaded[u.parity], loads(u))
                transpose_rows(l0, u, ("xT0", "xT1"), x_nat[:, u.parity], adj_nat[:, u.parity])

            def l0_m(u, l, c, starting=False):
                if c == 0 and l == 0:
                    pe.wait_ge(l0.act_took.sem, l0.act_took.at(u, "xT0"))
                    pe.wait_ge(l0.dve_took.sem, l0.dve_took.at(u, "xT0"))
                if c == 0 and l == 1:
                    pe.wait_ge(hT_ready.sem, hT_ready.at(u, "lo"))
                use = f"m{l}_{c}"
                if c > 0 or l > 0:
                    bank_free(l0, u, use)
                for side, mat in enumerate((LEFT[l], RIGHT[l])):
                    if starting and side == 1:
                        pe.wait_ge(weight_ready, mat + 1)
                    for t in range(HC):
                        if c == 0 and l == 0 and side == 0 and t == HC - 1:
                            pe.wait_ge(l0.act_took.sem, l0.act_took.at(u, "xT1"))
                            pe.wait_ge(l0.dve_took.sem, l0.dve_took.at(u, "xT1"))
                        last = split_product(bank0(use, side * COLS, (side + 1) * COLS),
                                             lambda h, t: w_half[h][:, mat, t, c * P:(c + 1) * P],
                                             lambda h, t: hT_half[h][:, t, :], [t])
                last.then_inc(l0.filled.sem, 1)

            def l0_lin(u, l, b, lender=None):
                use = f"lin{l}_{b}"
                bank_free(l0, u, use)
                if lender is not None:
                    pe.wait_ge(l1.dve_took.sem, l1.dve_took.at(lender, "v0"))
                split_product(bank0(use, 0, H), lambda h, t: hT_half[h][:, t, b * P:(b + 1) * P],
                              lambda h, t: w_half[h][:, LIN[l], t, :]).then_inc(l0.filled.sem, 1)

            def l0_u(u, l):
                use = f"u{l}"
                pe.wait_ge(l0.act_took.sem, l0.act_took.at(u, f"m{l}_1"))
                pe.wait_ge(l0.dve_took.sem, l0.dve_took.at(u, f"m{l}_1"))
                for b in range(BU):
                    for t in range(HC):
                        if b == 0 and t == HC - 1:
                            pe.wait_ge(l0.act_took.sem, l0.act_took.at(u, f"m{l}_{t}"))
                            pe.wait_ge(l0.dve_took.sem, l0.dve_took.at(u, f"m{l}_{t}"))
                        last = split_product(
                            bank0(use, b * COLS, (b + 1) * COLS).rearrange("p (s n) -> p s n", s=2),
                            lambda h, t: hT_half[h][:, t, b * P:(b + 1) * P],
                            lambda h, t: m_half[h][:, t, :, b * P:(b + 1) * P], [t])
                last.then_inc(l0.filled.sem, 1)

            def l0_ctx(u, l):
                pe.wait_ge(att_ready.sem, att_ready.at(u, f"layer{l}"))
                pe.wait_ge(l0.dve_took.sem, l0.dve_took.at(u, f"lin{l}_1"))
                for b in range(BU):
                    use = f"ctx{l}_{b}"
                    bank_free(l0, u, use)
                    pe.matmul(bank0(use, 0, H + 1), attT[:, b, :], lin[:, b, :], start=True,
                              stop=True).then_inc(l0.filled.sem, 1)

            def l0_hT(u):
                pe.wait_ge(normed.sem, normed.at(u, "ctx0_1"))
                pe.wait_ge(l0.dve_took.sem, l0.dve_took.at(u, "ctx0_1"))
                transpose_rows(l0, u, ("hT0", "hT1"), z)

            def l1_xT(u):
                pe.wait_ge(x1_ready.sem, x1_ready.at(u, "x1"))
                transpose_rows(l1, u, ("xT0", "xT1"), x1)

            def l1_qk(u, c):
                if c == 0:
                    pe.wait_ge(l1.act_took.sem, l1.act_took.at(u, "xT1"))
                    pe.wait_ge(l1.dve_took.sem, l1.dve_took.at(u, "xT1"))
                use = f"qk{c}"
                bank_free(l1, u, use)
                for side, mat in enumerate((WQ, WK)):
                    last = split_product(bank1(use, side * COLS, (side + 1) * COLS),
                                         lambda h, t: w_half[h][:, mat, t, c * P:(c + 1) * P],
                                         lambda h, t: xT_half[h][:, t, :])
                last.then_inc(l1.filled.sem, 1)

            def l1_s(u, b):
                for g0 in (0, 2):
                    if b > 0:
                        bank_free(l1, u, f"s{b}_{g0 + 1}")
                    for c in range(HC):
                        if b == 0 and g0 == 0:
                            pe.wait_ge(l1.act_took.sem, l1.act_took.at(u, f"qk{c}"))
                            pe.wait_ge(l1.dve_took.sem, l1.dve_took.at(u, f"qk{c}"))
                        for n, (lh, rh) in enumerate(((0, 0), (0, 1), (1, 0))):
                            for g in (g0, g0 + 1):
                                use = f"s{b}_{g}"
                                r = slice(g * D, (g + 1) * D)
                                mm = pe.matmul(bank1(use, c * P, (c + 1) * P),
                                               qk_half[lh][r, c, 0, b * P:(b + 1) * P],
                                               qk_half[rh][r, c, 1, b * P:(b + 1) * P],
                                               start=(n == 0), stop=(n == 2))
                                if c == HC - 1 and n == 2:
                                    mm.then_inc(l1.filled.sem, 1)

            def l1_v(u, b):
                use = f"v{b}"
                if b > 0:
                    bank_free(l1, u, use)
                split_product(bank1(use, 0, H), lambda h, t: xT_half[h][:, t, b * P:(b + 1) * P],
                              lambda h, t: w_half[h][:, WV, t, :]).then_inc(l1.filled.sem, 1)

            def l1_pT(u, b):
                pe.wait_ge(probs_scaled[b].sem, probs_scaled[b].at(u, f"graph{b}"))
                for c in range(HC):
                    use = f"pT{b}_{c}"
                    bank_free(l1, u, use)
                    for k in range(4):
                        last = pe.transpose(bank1(use, k * P, (k + 1) * P), probs[:, b, 4 * c + k, :], ident[:, :])
                    last.then_inc(l1.filled.sem, 1)

            def l1_oT(u, b):
                use = f"oT{b}"
                pe.wait_ge(l1.act_took.sem, l1.act_took.at(u, f"pT{b}_{HC - 1}"))
                if b == 0:
                    pe.wait_ge(l1.dve_took.sem, l1.dve_took.at(u, "v1"))
                bank_free(l1, u, use)
                for c in range(HC):
                    for g in range(GROUPS):
                        head = c * GROUPS + g
                        last = pe.matmul(psum[g * D:(g + 1) * D, l1.bank(use), c * P:(c + 1) * P],
                                         v[:, b, head * D:(head + 1) * D], probsT[:, b, g * HC + c, :],
                                         start=True, stop=True)
                last.then_inc(l1.filled.sem, 1)

            def l1_y(u, b):
                use = f"y{b}"
                pe.wait_ge(l1.act_took.sem, l1.act_took.at(u, f"oT{b}"))
                pe.wait_ge(l1.dve_took.sem, l1.dve_took.at(u, f"oT{b}"))
                bank_free(l1, u, use)
                split_product(bank1(use, 0, H), lambda h, t: oT_half[h][:, b, t, :],
                              lambda h, t: w_half[h][:, WO, t, :]).then_inc(l1.filled.sem, 1)

            def phase(a, b, c, more=True):
                if c is not None:
                    l1_pT(c, 0)
                l0_m(a, 0, 0)
                if c is not None:
                    l1_oT(c, 0)
                l0_m(a, 0, 1)
                if c is not None:
                    l1_pT(c, 1)
                l0_m(a, 0, 2)
                if c is not None:
                    l1_oT(c, 1)
                l0_lin(a, 0, 0)
                if c is not None:
                    l1_y(c, 0)
                    l1_y(c, 1)
                l1_xT(b)
                l0_u(a, 0)
                l0_lin(a, 0, 1)
                l1_qk(b, 0)
                l0_ctx(a, 0)
                l1_qk(b, 1)
                l1_qk(b, 2)
                l0_hT(a)
                l1_v(b, 0)
                l1_s(b, 0)
                l0_m(a, 1, 0)
                l1_s(b, 1)
                l0_m(a, 1, 1)
                l0_m(a, 1, 2)
                l0_lin(a, 1, 0, lender=b)
                l0_u(a, 1)
                l0_lin(a, 1, 1)
                l1_v(b, 1)
                l0_ctx(a, 1)
                if more:
                    l0_xT(following(a))

            def l1_end(c):
                l1_pT(c, 0)
                l1_oT(c, 0)
                l1_pT(c, 1)
                l1_oT(c, 1)
                l1_y(c, 0)
                l1_y(c, 1)

            pe.wait_ge(consts_ready, 1)
            a = even(0)
            l0_xT(a)
            for l in range(2):
                pe.wait_ge(weight_ready, LEFT[l] + 1)
                for c in range(HC):
                    l0_m(a, l, c, starting=c == 0)
                pe.wait_ge(weight_ready, LIN[l] + 1)
                l0_lin(a, l, 0)
                l0_u(a, l)
                l0_lin(a, l, 1)
                l0_ctx(a, l)
                if l == 0:
                    l0_hT(a)
            l0_xT(odd(0))
            pe.wait_ge(weight_ready, MATS)
            phase(odd(0), even(0), None)
            with pe.Fori(0, LOOPS - 1) as i:
                phase(even(i + 1), odd(i), even(i))
                phase(odd(i + 1), even(i + 1), odd(i))
            phase(even(LOOPS), odd(LOOPS - 1), even(LOOPS - 1))
            phase(odd(LOOPS), even(LOOPS), odd(LOOPS - 1), more=False)
            l1_end(even(LOOPS))
            b = odd(LOOPS)
            l1_xT(b)
            for c in range(HC):
                l1_qk(b, c)
            pe.wait_ge(normed.sem, normed.at(b, "ctx1_1"))
            l1_v(b, 0)
            l1_s(b, 0)
            l1_s(b, 1)
            l1_v(b, 1)
            l1_end(b)

        @block.scalar
        def _(act):
            def flat(t, k, n):
                return t[:, 2 * k:2 * k + n, :].rearrange("p c n -> p (c n)")

            def weight_high(w):
                act.wait_ge(weight_loaded[w % 3], 16 * (w // 3) + 16)
                act.activation(w_hi[:, w].rearrange("p c n -> p (c n)"), stage[:, w % 3, :], ACT.Copy,
                               scale=W_SCALE).then_inc(weight_hi_ready, 1)

            def l0_xT(u):
                act.wait_ge(l0.filled.sem, l0.filled.at(u, "xT0"))
                act.activation(flat(hT_hi, 0, 2), bank0("xT0"), ACT.Copy).then_inc(l0.act_took.sem, 1)
                act.wait_ge(l0.filled.sem, l0.filled.at(u, "xT1"))
                act.activation(flat(hT_hi, 1, 1), bank0("xT1", 0, COLS), ACT.Copy).then_inc(l0.act_took.sem, 1)

            def l0_adjT(u):
                act.wait_ge(l0.dve_took.sem, l0.dve_took.at(u, "xT1"))
                act.activation(adjT[:, :, :].rearrange("p b n -> p (b n)"), bank0("xT1", COLS), ACT.Copy)\
                   .then_inc(adjT_ready.sem, 1)

            def l0_m(u, l, c):
                act.wait_ge(l0.filled.sem, l0.filled.at(u, f"m{l}_{c}"))
                act.activation(m_hi[:, c].rearrange("p s n -> p (s n)"), bank0(f"m{l}_{c}"), ACT.Copy)\
                   .then_inc(l0.act_took.sem, 1)

            def l0_exp(u, l):
                act.wait_ge(scores_ready.sem, scores_ready.at(u, f"layer{l}"))
                act.activation(expT[:, :, :], scoreT[:, :, :], ACT.Exp, scale=1.0 / (W_SCALE * TEMPER))\
                   .then_inc(exp_ready.sem, 1)

            def l0_norm(u, l):
                act.wait_ge(coef_ready.sem, coef_ready.at(u, f"layer{l}"))
                for b in range(BU):
                    act.activation(z[:, b, :], bank0(f"ctx{l}_{b}", 0, H), ACT.Identity,
                                   bias=ln_shift[:, b:b + 1], scale=ln_scale[:, b:b + 1])\
                       .then_inc(normed.sem, 1)

            def l0_hT(u):
                for k, use in enumerate(("hT0", "hT1")):
                    act.wait_ge(l0.filled.sem, l0.filled.at(u, use))
                    for c in range(2 * k, min(2 * k + 2, HC)):
                        last = act.activation(h_T[:, c, :], bank0(use, c % 2 * COLS, (c % 2 + 1) * COLS), ACT.Relu,
                                              bias=ln_col[:, 1, c:c + 1], scale=ln_col[:, 0, c:c + 1])
                    last.then_inc(l0.act_took.sem, 1)

            def l0_x1(u):
                act.wait_ge(coef_ready.sem, coef_ready.at(u, "x1"))
                for b in range(BU):
                    last = act.activation(x1[:, b, :], y[:, b, :], ACT.Identity,
                                          bias=ln_shift[:, b:b + 1], scale=ln_scale[:, b:b + 1])
                last.then_inc(x1_ready.sem, 1)

            def l1_xT(u):
                for k, use in enumerate(("xT0", "xT1")):
                    n = 2 - k
                    act.wait_ge(l1.filled.sem, l1.filled.at(u, use))
                    act.activation(flat(xT_hi, k, n), bank1(use, 0, n * COLS), ACT.Copy)\
                       .then_inc(l1.act_took.sem, 1)

            def l1_qk(u, c):
                act.wait_ge(l1.filled.sem, l1.filled.at(u, f"qk{c}"))
                act.activation(qk_hi[:, c].rearrange("p s n -> p (s n)"), bank1(f"qk{c}"), ACT.Copy)\
                   .then_inc(l1.act_took.sem, 1)

            def l1_exp(u, b, part):
                if part == 0:
                    act.wait_ge(max_ready.sem, max_ready.at(u, f"graph{b}"))
                for k in range(3 * part, 3 * part + 3):
                    last = act.activation(probs[:, b, k, :], scores[:, b, k, :], ACT.Exp,
                                          bias=minus_max[:, b, k:k + 1], accum_out=prob_sum[:, b, k:k + 1])
                if part == 3:
                    last.then_inc(probs_ready.sem, 1)

            def l1_pT(u, b):
                for c in range(HC):
                    act.wait_ge(l1.filled.sem, l1.filled.at(u, f"pT{b}_{c}"))
                    act.activation(probsT[:, b, 4 * c:4 * c + 4, :].rearrange("p k n -> p (k n)"),
                                   bank1(f"pT{b}_{c}"), ACT.Copy).then_inc(l1.act_took.sem, 1)

            def l1_oT(u, b):
                act.wait_ge(l1.filled.sem, l1.filled.at(u, f"oT{b}"))
                act.activation(oT_hi[:, b].rearrange("p c n -> p (c n)"), bank1(f"oT{b}", 0, H), ACT.Copy)\
                   .then_inc(l1.act_took.sem, 1)

            def l1_result(u):
                act.wait_ge(coef2_ready.sem, coef2_ready.at(u, "y2"))
                if not u.first:
                    act.wait_ge(result_stored, 16 * u.n)
                for b in range(BU):
                    last = act.activation(result[:, b, :], y2[:, b, :], ACT.Identity,
                                          bias=ln_shift2[:, b:b + 1], scale=root2[:, b:b + 1])
                last.then_inc(result_ready.sem, 1)

            def phase(a, b, c, more=True):
                if c is not None:
                    l1_pT(c, 0)
                l0_adjT(a)
                l0_norm(b, 1)
                l0_m(a, 0, 0)
                if c is not None:
                    l1_oT(c, 0)
                l0_m(a, 0, 1)
                if c is not None:
                    l1_pT(c, 1)
                l0_m(a, 0, 2)
                if c is not None:
                    l1_oT(c, 1)
                l0_x1(b)
                l1_xT(b)
                l0_exp(a, 0)
                l1_qk(b, 0)
                if c is not None:
                    l1_result(c)
                l0_norm(a, 0)
                l1_qk(b, 1)
                l1_qk(b, 2)
                l0_hT(a)
                l0_m(a, 1, 0)
                l1_exp(b, 0, 0)
                l1_exp(b, 0, 1)
                l0_m(a, 1, 1)
                l1_exp(b, 0, 2)
                l0_m(a, 1, 2)
                l1_exp(b, 0, 3)
                l1_exp(b, 1, 0)
                l1_exp(b, 1, 1)
                l0_exp(a, 1)
                l1_exp(b, 1, 2)
                l1_exp(b, 1, 3)
                if more:
                    l0_xT(following(a))

            def l1_end(c):
                l1_pT(c, 0)
                l1_oT(c, 0)
                l1_pT(c, 1)
                l1_oT(c, 1)
                l1_result(c)

            a = even(0)
            weight_high(0)
            l0_xT(a)
            weight_high(1)
            l0_adjT(a)
            weight_high(2)
            for c in range(HC):
                l0_m(a, 0, c)
                weight_high(3 + c)
            l0_exp(a, 0)
            weight_high(6)
            weight_high(7)
            l0_norm(a, 0)
            act.wait_ge(rows_loaded, 32)
            l0_hT(a)
            weight_high(8)
            l0_m(a, 1, 0)
            weight_high(9)
            l0_m(a, 1, 1)
            l0_m(a, 1, 2)
            l0_exp(a, 1)
            l0_xT(odd(0))
            phase(odd(0), even(0), None)
            with act.Fori(0, LOOPS - 1) as i:
                phase(even(i + 1), odd(i), even(i))
                phase(odd(i + 1), even(i + 1), odd(i))
            phase(even(LOOPS), odd(LOOPS - 1), even(LOOPS - 1))
            phase(odd(LOOPS), even(LOOPS), odd(LOOPS - 1), more=False)
            b = odd(LOOPS)
            c = even(LOOPS)
            l1_pT(c, 0)
            l0_norm(b, 1)
            l1_oT(c, 0)
            l1_pT(c, 1)
            l1_oT(c, 1)
            l0_x1(b)
            l1_xT(b)
            l1_result(c)
            for k in range(HC):
                l1_qk(b, k)
            for g in range(BU):
                for part in range(4):
                    l1_exp(b, g, part)
            l1_end(b)

        @block.vector
        def _(dve):
            def flat(t, k, n):
                return t[:, 2 * k:2 * k + n, :].rearrange("p c n -> p (c n)")

            def weight_low(w):
                dve.wait_ge(weight_hi_ready, w + 1)
                dve.scalar_tensor_tensor(out=w_lo[:, w].rearrange("p c n -> p (c n)"), in0=stage[:, w % 3, :],
                                         scalar=W_SCALE, in1=w_hi[:, w].rearrange("p c n -> p (c n)"),
                                         op0=ALU.mult, op1=ALU.subtract).then_inc(weight_ready, 1)

            def low_half(banks, unit, use, lo, hi, n):
                dve.wait_ge(banks.act_took.sem, banks.act_took.at(unit, use))
                dve.tensor_tensor(lo, psum[:, banks.bank(use), 0:n], hi, ALU.subtract)\
                   .then_inc(banks.dve_took.sem, 1)

            def l0_xT(u):
                for k, use in enumerate(("xT0", "xT1")):
                    low_half(l0, u, use, flat(hT_lo, k, 2 - k), flat(hT_hi, k, 2 - k), (2 - k) * COLS)

            def l0_m(u, l, c):
                low_half(l0, u, f"m{l}_{c}", m_lo[:, c].rearrange("p s n -> p (s n)"),
                         m_hi[:, c].rearrange("p s n -> p (s n)"), 2 * COLS)

            def l0_lin(u, l, b):
                dve.wait_ge(l0.filled.sem, l0.filled.at(u, f"lin{l}_{b}"))
                dve.tensor_tensor(lin[:, b, 0:H], bank0(f"lin{l}_{b}", 0, H), row[:, B_LIN[l], :], ALU.add)\
                   .then_inc(l0.dve_took.sem, 1)

            def l0_scores(u, l):
                if l == 0:
                    dve.wait_ge(masks_ready.sem, masks_ready.at(u, "masks"))
                dve.wait_ge(l0.filled.sem, l0.filled.at(u, f"u{l}"))
                dve.tensor_tensor(masked[:, :, :, :].rearrange("p b s n -> p (b s n)"), bank0(f"u{l}"),
                                  side_mask[:, :, :, :].rearrange("p b s n -> p (b s n)"), ALU.mult)\
                   .then_inc(l0.dve_took.sem, 1)
                dve.wait_ge(l0.dve_took.sem, l0.dve_took.at(u, f"u{l}"))
                dve.tensor_tensor(scoreT[:, :, :], masked[:, :, 0, :], masked[:, :, 1, :], ALU.add)\
                   .then_inc(scores_ready.sem, 1)

            def l0_att(u, l):
                dve.wait_ge(exp_ready.sem, exp_ready.at(u, f"layer{l}"))
                dve.tensor_tensor(attT[:, :, :], expT[:, :, :], adjT[:, :, :], ALU.mult).then_inc(att_ready.sem, 1)

            def l0_stats(u, l):
                for b in range(BU):
                    dve.wait_ge(l0.filled.sem, l0.filled.at(u, f"ctx{l}_{b}"))
                    last = dve.bn_stats(stats[:, b, :], bank0(f"ctx{l}_{b}", 0, H))
                    if b == BU - 1:
                        last.then_inc(l0_own.sem, 1)
                    dve.tensor_scalar(eps_term[:, b:b + 1], bank0(f"ctx{l}_{b}", H, H + 1), 1e-3,
                                      W_SCALE * 1e-3 * 1e-10, ALU.mult, ALU.add).then_inc(l0.dve_took.sem, 1)

            def l0_moments(u, l):
                moments_of(l0_own, u, f"stats{l}", stats, moments, var_ready.sem)

            def moments_of(own, u, step, source, target, done):
                dve.wait_ge(own.sem, own.at(u, step))
                dve.memset(pause[:, :], 0.0)
                for b in range(BU):
                    last = dve.bn_aggr(target[:, b, :], source[:, b, :])
                last.then_inc(done, 1)

            def l0_coef(u, l):
                dve.wait_ge(root_ready.sem, root_ready.at(u, f"layer{l}"))
                dve.wait_ge(l0.dve_took.sem, l0.dve_took.at(u, f"ctx{l}_1"))
                dve.scalar_tensor_tensor(out=spread[:, :], in0=root[:, :], scalar=UNBIAS, in1=eps_term[:, :],
                                         op0=ALU.mult, op1=ALU.add).then_inc(l0_own.sem, 1)
                dve.wait_ge(l0_own.sem, l0_own.at(u, f"spread{l}"))
                dve.reciprocal(ln_scale[:, :], spread[:, :]).then_inc(l0_own.sem, 1)
                dve.wait_ge(l0_own.sem, l0_own.at(u, f"scale{l}"))
                dve.scalar_tensor_tensor(out=ln_shift[:, :], in0=moments[:, :, 0], scalar=-1.0, in1=ln_scale[:, :],
                                         op0=ALU.mult, op1=ALU.mult).then_inc(coef_ready.sem, 1)

            def l0_hT(u):
                dve.wait_ge(l0.act_took.sem, l0.act_took.at(u, "hT1"))
                dve.tensor_copy(hT_hi[:, :, :], h_T[:, :, :]).then_inc(hT_ready.sem, 1)
                dve.wait_ge(hT_ready.sem, hT_ready.at(u, "hi"))
                dve.tensor_tensor(hT_lo[:, :, :], h_T[:, :, :], hT_hi[:, :, :], ALU.subtract)\
                   .then_inc(hT_ready.sem, 1)

            def l0_y(u):
                dve.wait_ge(gain_ready.sem, gain_ready.at(u, "scaled"))
                dve.tensor_tensor(shifted[:, :, :], scaled[:, :, :],
                                  row[:, LN_B1:LN_B1 + 1, :].to_broadcast([P, BU, H]), ALU.add)\
                   .then_inc(l0_own.sem, 1)
                dve.wait_ge(l0_own.sem, l0_own.at(u, "shifted"))
                dve.scalar_tensor_tensor(out=y[:, :, :], in0=shifted[:, :, :], scalar=0.0,
                                         in1=x_nat[:, u.parity, :, :], op0=ALU.max, op1=ALU.add)\
                   .then_inc(l0_own.sem, 1)
                dve.wait_ge(l0_own.sem, l0_own.at(u, "y"))
                for b in range(BU):
                    last = dve.bn_stats(stats[:, b, :], y[:, b, :])
                last.then_inc(l0_own.sem, 1)
                moments_of(l0_own, u, "ystats", stats, moments, l0_own.sem)
                dve.wait_ge(l0_own.sem, l0_own.at(u, "ymoments"))
                dve.tensor_scalar(spread[:, :], moments[:, :, 1], 1e-5, None, ALU.add).then_inc(var_ready.sem, 1)

            def l0_y_coef(u):
                dve.wait_ge(root_ready.sem, root_ready.at(u, "x1"))
                dve.tensor_copy(ln_scale[:, :], root[:, :])
                dve.scalar_tensor_tensor(out=ln_shift[:, :], in0=moments[:, :, 0], scalar=-1.0, in1=root[:, :],
                                         op0=ALU.mult, op1=ALU.mult).then_inc(coef_ready.sem, 1)

            def l1_xT(u):
                for k, use in enumerate(("xT0", "xT1")):
                    low_half(l1, u, use, flat(xT_lo, k, 2 - k), flat(xT_hi, k, 2 - k), (2 - k) * COLS)

            def l1_qk(u, c):
                low_half(l1, u, f"qk{c}", qk_lo[:, c].rearrange("p s n -> p (s n)"),
                         qk_hi[:, c].rearrange("p s n -> p (s n)"), 2 * COLS)

            def l1_scores(u, b):
                if b == 0:
                    dve.wait_ge(adj_loaded[u.parity], loads(u))
                bias = adj_nat[:, u.parity, b, :].unsqueeze(1).to_broadcast([P, HC, P])
                for g in range(GROUPS):
                    use = f"s{b}_{g}"
                    dve.wait_ge(l1.filled.sem, l1.filled.at(u, use))
                    dve.scalar_tensor_tensor(out=scores[:, b, g * HC:(g + 1) * HC, :],
                                             in0=bank1(use, 0, H).rearrange("p (c n) -> p c n", c=HC),
                                             scalar=SCALE / (W_SCALE * W_SCALE), in1=bias,
                                             op0=ALU.mult, op1=ALU.add).then_inc(l1.dve_took.sem, 1)

            def l1_scale_probs(u, b):
                dve.wait_ge(prob_scale_ready.sem, prob_scale_ready.at(u, f"graph{b}"))
                dve.tensor_tensor(probs[:, b, :, :], probs[:, b, :, :],
                                  prob_scale[:, b, :].unsqueeze(2).to_broadcast([P, HEADS, P]), ALU.mult)\
                   .then_inc(probs_scaled[b].sem, 1)

            def l1_max(u, b):
                dve.wait_ge(l1.dve_took.sem, l1.dve_took.at(u, f"s{b}_3"))
                dve.tensor_reduce(minus_max[:, b, :], scores[:, b, :, :], AX, ALU.max, negate=True)\
                   .then_inc(max_ready.sem, 1)

            def l1_min(u, b):
                dve.tensor_reduce(minimum[:, b, :], scores[:, b, :, :], AX, ALU.min).then_inc(l1_own.sem, 1)
                dve.wait_ge(max_ready.sem, max_ready.at(u, f"graph{b}"))
                dve.tensor_scalar(max_nonzero[:, b, :], minus_max[:, b, :], 0.0, None, ALU.not_equal)\
                   .then_inc(l1_own.sem, 1)
                dve.wait_ge(l1_own.sem, l1_own.at(u, f"nonzero{b}"))
                dve.scalar_tensor_tensor(out=live[:, b, :], in0=minimum[:, b, :], scalar=0.0,
                                         in1=max_nonzero[:, b, :], op0=ALU.not_equal, op1=ALU.max)\
                   .then_inc(l1_own.sem, 1)

            def l1_prob_scale(u, b):
                dve.wait_ge(probs_ready.sem, probs_ready.at(u, f"graph{b}"))
                dve.reciprocal(inverse_sum[:, b, :], prob_sum[:, b, :]).then_inc(l1_own.sem, 1)
                dve.wait_ge(l1_own.sem, l1_own.at(u, f"inverse{b}"))
                dve.scalar_tensor_tensor(out=prob_scale[:, b, :], in0=live[:, b, :], scalar=1.0 / W_SCALE,
                                         in1=inverse_sum[:, b, :], op0=ALU.mult, op1=ALU.mult)\
                   .then_inc(prob_scale_ready.sem, 1)

            def l1_v(u, b):
                dve.wait_ge(l1.filled.sem, l1.filled.at(u, f"v{b}"))
                dve.tensor_tensor(v[:, b, :], bank1(f"v{b}", 0, H), row[:, BV, :], ALU.add)\
                   .then_inc(l1.dve_took.sem, 1)

            def l1_oT(u, b):
                low_half(l1, u, f"oT{b}", oT_lo[:, b].rearrange("p c n -> p (c n)"),
                         oT_hi[:, b].rearrange("p c n -> p (c n)"), H)

            def l1_y(u, b):
                if b == 0:
                    dve.wait_ge(residual_ready.sem, residual_ready.at(u, "residual"))
                dve.wait_ge(l1.filled.sem, l1.filled.at(u, f"y{b}"))
                dve.scalar_tensor_tensor(out=y2[:, b, :], in0=bank1(f"y{b}", 0, H), scalar=1.0 / W_SCALE,
                                         in1=residual[:, b, :], op0=ALU.mult, op1=ALU.add)\
                   .then_inc(l1.dve_took.sem, 1)

            def l1_stats(u):
                dve.wait_ge(l1.dve_took.sem, l1.dve_took.at(u, "y1"))
                for b in range(BU):
                    last = dve.bn_stats(stats2[:, b, :], y2[:, b, :])
                last.then_inc(l1_own.sem, 1)
                moments_of(l1_own, u, "stats2", stats2, moments2, l1_own.sem)
                dve.wait_ge(l1_own.sem, l1_own.at(u, "moments2"))
                dve.tensor_scalar(variance2[:, :], moments2[:, :, 1], 1e-5, None, ALU.add)\
                   .then_inc(var2_ready.sem, 1)

            def l1_coef(u):
                dve.wait_ge(root2_ready.sem, root2_ready.at(u, "y2"))
                dve.scalar_tensor_tensor(out=ln_shift2[:, :], in0=moments2[:, :, 0], scalar=-1.0, in1=root2[:, :],
                                         op0=ALU.mult, op1=ALU.mult).then_inc(coef2_ready.sem, 1)

            def phase(a, b, c, more=True):
                l0_m(a, 0, 0)
                if c is not None:
                    l1_oT(c, 0)
                l0_y(b)
                l0_m(a, 0, 1)
                l0_y_coef(b)
                if c is not None:
                    l1_oT(c, 1)
                l0_m(a, 0, 2)
                l0_lin(a, 0, 0)
                if c is not None:
                    l1_y(c, 0)
                    l1_y(c, 1)
                    l1_stats(c)
                l1_xT(b)
                l0_scores(a, 0)
                if c is not None:
                    l1_coef(c)
                l0_att(a, 0)
                l0_lin(a, 0, 1)
                l0_stats(a, 0)
                l0_moments(a, 0)
                l1_qk(b, 0)
                l0_coef(a, 0)
                l1_qk(b, 1)
                l1_qk(b, 2)
                l0_hT(a)
                l1_v(b, 0)
                l1_scores(b, 0)
                l1_max(b, 0)
                l0_m(a, 1, 0)
                l1_scores(b, 1)
                l1_max(b, 1)
                l0_m(a, 1, 1)
                l0_m(a, 1, 2)
                l1_min(b, 0)
                l0_lin(a, 1, 0)
                l0_scores(a, 1)
                l1_prob_scale(b, 0)
                l0_lin(a, 1, 1)
                l0_att(a, 1)
                l1_min(b, 1)
                l0_stats(a, 1)
                if more:
                    l0_xT(following(a))
                l0_moments(a, 1)
                l1_v(b, 1)
                l1_prob_scale(b, 1)
                l0_coef(a, 1)
                l1_scale_probs(b, 1)

            def l1_end(c):
                l1_oT(c, 0)
                l1_oT(c, 1)
                l1_y(c, 0)
                l1_y(c, 1)
                l1_stats(c)
                l1_coef(c)

            dve.memset(lin[:, :, H:H + 1], W_SCALE)
            a = even(0)
            weight_low(0)
            l0_xT(a)
            weight_low(1)
            weight_low(2)
            dve.wait_ge(rows_loaded, 32)
            for r in (*B_LIN, BV):
                last = dve.tensor_scalar(row[:, r, :], row[:, r, :], W_SCALE, None, ALU.mult)
            last.then_inc(rows_ready, 1)
            l0_m(a, 0, 0)
            weight_low(3)
            l0_m(a, 0, 1)
            weight_low(4)
            l0_m(a, 0, 2)
            dve.wait_ge(rows_ready, 1)
            for l in range(2):
                if l == 1:
                    l0_coef(a, 0)
                    weight_low(6)
                    l0_hT(a)
                    weight_low(7)
                    l0_m(a, 1, 0)
                    weight_low(8)
                    l0_m(a, 1, 1)
                    l0_m(a, 1, 2)
                l0_lin(a, l, 0)
                l0_scores(a, l)
                l0_lin(a, l, 1)
                l0_att(a, l)
                weight_low(5 if l == 0 else 9)
                l0_stats(a, l)
                l0_moments(a, l)
            l0_xT(odd(0))
            l0_coef(a, 1)
            phase(odd(0), even(0), None)
            with dve.Fori(0, LOOPS - 1) as i:
                phase(even(i + 1), odd(i), even(i))
                phase(odd(i + 1), even(i + 1), odd(i))
            phase(even(LOOPS), odd(LOOPS - 1), even(LOOPS - 1))
            phase(odd(LOOPS), even(LOOPS), odd(LOOPS - 1), more=False)
            b = odd(LOOPS)
            c = even(LOOPS)
            l1_oT(c, 0)
            l0_y(b)
            l1_oT(c, 1)
            l0_y_coef(b)
            l1_y(c, 0)
            l1_y(c, 1)
            l1_xT(b)
            l1_stats(c)
            l1_coef(c)
            for k in range(HC):
                l1_qk(b, k)
            l1_v(b, 0)
            l1_scores(b, 0)
            l1_max(b, 0)
            l1_scores(b, 1)
            l1_max(b, 1)
            l1_min(b, 0)
            l1_prob_scale(b, 0)
            l1_min(b, 1)
            l1_v(b, 1)
            l1_prob_scale(b, 1)
            l1_scale_probs(b, 1)
            l1_end(b)

        @block.gpsimd
        def _(pool):
            def l0_masks(u):
                pool.wait_ge(adjT_ready.sem, adjT_ready.at(u, "xT1"))

                pool.tensor_tensor(side_mask[:, :, 0, :], adjT[:, :, :],
                                   tri_left[:, :].unsqueeze(1).to_broadcast([P, BU, P]), ALU.mult)
                pool.tensor_tensor(side_mask[:, :, 1, :], adj_nat[:, u.parity, :, :],
                                   tri_right[:, :].unsqueeze(1).to_broadcast([P, BU, P]), ALU.mult)\
                    .then_inc(masks_ready.sem, 1)

            def l0_root(u, l):
                pool.wait_ge(var_ready.sem, var_ready.at(u, f"layer{l}"))
                pool.tensor_tensor(root[:, :], moments[:, :, 1], half_power[:, :], ALU.pow)\
                    .then_inc(root_ready.sem, 1)

            def l0_gain(u):
                pool.wait_ge(normed.sem, normed.at(u, "ctx1_1"))
                pool.tensor_tensor(scaled[:, :, :], z[:, :, :],
                                   row[:, LN_A1:LN_A1 + 1, :].to_broadcast([P, BU, H]), ALU.mult)\
                    .then_inc(gain_ready.sem, 1)

            def l0_y_root(u):
                pool.wait_ge(var_ready.sem, var_ready.at(u, "x1"))
                pool.tensor_tensor(root[:, :], spread[:, :], minus_half_power[:, :], ALU.pow)\
                    .then_inc(root_ready.sem, 1)

            def l1_residual(u):
                pool.wait_ge(x1_ready.sem, x1_ready.at(u, "x1"))
                if not u.first:
                    pool.wait_ge(l1.dve_took.sem, l1.dve_took.at(u, "y1", back=1))
                pool.tensor_tensor(residual[:, :, :], x1[:, :, :],
                                   row[:, BO:BO + 1, :].to_broadcast([P, BU, H]), ALU.add)\
                    .then_inc(residual_ready.sem, 1)

            def l1_scale_probs(u, b):
                pool.wait_ge(prob_scale_ready.sem, prob_scale_ready.at(u, f"graph{b}"))
                pool.tensor_tensor(probs[:, b, :, :], probs[:, b, :, :],
                                   prob_scale[:, b, :].unsqueeze(2).to_broadcast([P, HEADS, P]), ALU.mult)\
                    .then_inc(probs_scaled[b].sem, 1)

            def l1_root(u):
                pool.wait_ge(var2_ready.sem, var2_ready.at(u, "y2"))
                pool.tensor_tensor(root2[:, :], variance2[:, :], minus_half_power[:, :], ALU.pow)\
                    .then_inc(root2_ready.sem, 1)

            def phase(a, b, c):
                l0_gain(b)
                l0_y_root(b)
                l0_masks(a)
                if c is not None:
                    l1_root(c)
                l1_residual(b)
                l0_root(a, 0)
                l1_scale_probs(b, 0)
                l0_root(a, 1)

            pool.memset(ident[:, :], 0.0)
            pool.memset(tri_left[:, :], 1.0)
            pool.memset(tri_right[:, :], 1.0)
            pool.memset(half_power[:, :], 0.5)
            pool.memset(minus_half_power[:, :], -0.5).then_inc(const_set, 1)
            pool.wait_ge(const_set, 1)
            pool.affine_select(out=tri_left[:, :], in_=tri_left[:, :], compare_op=ALU.is_ge, fill=0.0, base=0,
                               pattern=[[-1, P]], channel_multiplier=1)
            pool.affine_select(out=tri_right[:, :], in_=tri_right[:, :], compare_op=ALU.is_gt, fill=0.0, base=0,
                               pattern=[[1, P]], channel_multiplier=-1)
            pool.affine_select(out=ident[:, :], in_=ident[:, :], compare_op=ALU.not_equal, fill=1.0, base=0,
                               pattern=[[-1, P]], channel_multiplier=1).then_inc(consts_ready, 1)
            pool.wait_ge(consts_ready, 1)
            a = even(0)
            pool.wait_ge(adj_loaded[a.parity], loads(a))
            l0_masks(a)
            l0_root(a, 0)
            l0_root(a, 1)
            pool.wait_ge(rows_loaded, 32)
            pool.wait_ge(adj_loaded[1], 16)
            phase(odd(0), even(0), None)
            with pool.Fori(0, LOOPS - 1) as i:
                phase(even(i + 1), odd(i), even(i))
                phase(odd(i + 1), even(i + 1), odd(i))
            phase(even(LOOPS), odd(LOOPS - 1), even(LOOPS - 1))
            phase(odd(LOOPS), even(LOOPS), odd(LOOPS - 1))
            b = odd(LOOPS)
            l0_gain(b)
            l0_y_root(b)
            l1_root(even(LOOPS))
            l1_residual(b)
            l1_scale_probs(b, 0)
            l1_root(b)


def kernel(x, adj, L0_gnn_W_left, L0_gnn_W_right, L0_gnn_W_lin, L0_gnn_b_lin, L0_gnn_ln_a, L0_gnn_ln_b,
           L1_gnn_Wq, L1_gnn_Wk, L1_gnn_Wv, L1_gnn_bv, L1_gnn_Wo, L1_gnn_bo):
    import numpy as np
    import concourse.bacc as bacc
    from concourse import mybir as _mybir
    from concourse.bass_utils import run_bass_kernel_spmd

    x, adj = np.ascontiguousarray(x), np.ascontiguousarray(adj)
    H = x.shape[-1]
    HC = H // 128
    wl, wr, wn = (np.asarray(w) for w in (L0_gnn_W_left, L0_gnn_W_right, L0_gnn_W_lin))
    mats = [wl[0].T, wr[0].T, wn[0], wl[1].T, wr[1].T, wn[1]]
    mats += [np.asarray(w) for w in (L1_gnn_Wq, L1_gnn_Wk, L1_gnn_Wv, L1_gnn_Wo)]
    stacked = np.stack(mats).transpose(2, 0, 1).reshape(HC, 128, len(mats), H)
    weights = np.ascontiguousarray(stacked.transpose(1, 2, 0, 3)).reshape(128, len(mats), HC * H)
    b_lin, ln_a, ln_b = (np.asarray(t) for t in (L0_gnn_b_lin, L0_gnn_ln_a, L0_gnn_ln_b))
    rows = np.ascontiguousarray(np.stack([b_lin[0], b_lin[1], ln_a[1], ln_b[1],
                                          np.asarray(L1_gnn_bv), np.asarray(L1_gnn_bo)]))
    cols = np.ascontiguousarray(np.stack([ln_a[0], ln_b[0]]).reshape(2, HC, 128).transpose(2, 0, 1))

    nc = bacc.Bacc("TRN2", target_bir_lowering=False, num_devices=1)
    arrays = {"x_dram": x, "adj_dram": adj, "weights_dram": weights, "rows_dram": rows, "cols_dram": cols}
    args = [nc.dram_tensor(name, a.shape, _mybir.dt.from_np(a.dtype), kind="ExternalInput").ap()
            for name, a in arrays.items()]
    out = nc.dram_tensor("out_dram", x.shape, _mybir.dt.from_np(x.dtype), kind="ExternalOutput").ap()
    graph_net_kernel(nc, *args, out)
    return run_bass_kernel_spmd(nc, [arrays], core_ids=[0]).results[0]["out_dram"]
```
